# Optimizing a Trainium2 kernel written in Bass

```python
import numpy as np
import jax
import jax.numpy as jnp

def _softmax(x, axis=-1):
    return jax.nn.softmax(x, axis=axis)
def _gelu(x):
    return jax.nn.gelu(x, approximate=True)
def _silu(x):
    return jax.nn.silu(x)
def _sigmoid(x):
    return jax.nn.sigmoid(x)
def _layernorm(x, axis=-1, eps=1e-5):
    m = jnp.mean(x, axis=axis, keepdims=True)
    v = jnp.var(x, axis=axis, keepdims=True)
    return (x - m) / jnp.sqrt(v + eps)
def _scatter_add(tgt, idx, src, axis=0):
    return tgt.at[idx].add(src)
def _segment_sum(src, seg, n):
    return jax.ops.segment_sum(src, seg, n)

kernel_name = 'mk_adj_resnorm_d2_adj_256_531f40'

def setup_inputs(seed: int = 0):
    np.random.seed(seed)
    _w = jnp.asarray
    def _rec_inputs():
        import jax
        import jax.numpy as jnp
        _gk = jax.random.key(seed)
        x = -0.0005146 + 1 * jax.random.normal(jax.random.fold_in(_gk, 1), (8, 2048, 256), jnp.float32)
        _a = jax.random.bernoulli(jax.random.fold_in(_gk, 2), 0.00390625, (8, 2048, 2048))
        adj = _a.astype(jnp.int32)
        return x, adj
    x, adj = _rec_inputs()
    def _L0_gnn_setup():
        import jax, jax.numpy as jnp
        import numpy as np
        B, N, C, OUT, S = (4, 2048, 256, 256, 25)
        DENSITY = 0.008
        key = jax.random.key(seed)
        kA, kX, kW = jax.random.split(key, 3)
        A = jax.random.bernoulli(kA, DENSITY, (B, N, N)).astype(jnp.int32)
        X = jax.random.normal(kX, (B, N, C), dtype=jnp.float32)
        W = jax.random.normal(kW, (2 * C, OUT), dtype=jnp.float32) * np.float32(1.0 / np.sqrt(2 * C))
        b = jnp.zeros((OUT,), dtype=jnp.float32)
        return {'A': A, 'X': X, 'W': W, 'b': b}
    _L0_gnn_all = _L0_gnn_setup()
    _L0_gnn_in = {k: v for k, v in _L0_gnn_all.items() if k in ('W', 'b', )}
    del _L0_gnn_all

    def _L1_gnn_setup():
        import jax, jax.numpy as jnp
        import numpy as np
        B, N, IN_F, OUT_F, H, NUM_EDGE_TYPES = (16, 512, 256, 256, 8, 50)
        HEAD_DIM = OUT_F // H
        LN_EPS = 1e-05
        key = jax.random.key(seed)
        ks = jax.random.split(key, 8)
        x = jax.random.normal(ks[0], (B, N, IN_F), dtype=jnp.float32)
        adj = jax.random.randint(ks[1], (B, N, N), 0, 2, dtype=jnp.int32)
        edge_types = jax.random.randint(ks[2], (B, N, N), 0, NUM_EDGE_TYPES, dtype=jnp.int32)
        W = jax.random.normal(ks[3], (IN_F, OUT_F), dtype=jnp.float32) / np.sqrt(IN_F)
        a1 = jax.random.normal(ks[4], (HEAD_DIM,), dtype=jnp.float32) / np.sqrt(HEAD_DIM)
        a2 = jax.random.normal(ks[5], (HEAD_DIM,), dtype=jnp.float32) / np.sqrt(HEAD_DIM)
        edge_emb = jax.random.normal(ks[6], (NUM_EDGE_TYPES, H), dtype=jnp.float32) * 0.02
        edge_emb = edge_emb.at[0].set(0.0)
        ln_gamma = jnp.ones((OUT_F,), dtype=jnp.float32)
        ln_beta = jnp.zeros((OUT_F,), dtype=jnp.float32)
        return {'x': x, 'adj': adj, 'edge_types': edge_types, 'W': W, 'a1': a1, 'a2': a2, 'edge_emb': edge_emb, 'ln_gamma': ln_gamma, 'ln_beta': ln_beta}
    _L1_gnn_all = _L1_gnn_setup()
    _L1_gnn_in = {k: v for k, v in _L1_gnn_all.items() if k in ('W', 'a1', 'a2', 'edge_emb', 'ln_gamma', 'ln_beta', )}
    del _L1_gnn_all

    return {
        "x": x,
        "adj": adj,
        "L0_gnn_W": _L0_gnn_in["W"],
        "L0_gnn_b": _L0_gnn_in["b"],
        "L1_gnn_W": _L1_gnn_in["W"],
        "L1_gnn_a1": _L1_gnn_in["a1"],
        "L1_gnn_a2": _L1_gnn_in["a2"],
        "L1_gnn_edge_emb": _L1_gnn_in["edge_emb"],
        "L1_gnn_ln_gamma": _L1_gnn_in["ln_gamma"],
        "L1_gnn_ln_beta": _L1_gnn_in["ln_beta"],
    }

def reference(x, adj, L0_gnn_W, L0_gnn_b, L1_gnn_W, L1_gnn_a1, L1_gnn_a2, L1_gnn_edge_emb, L1_gnn_ln_gamma, L1_gnn_ln_beta):
    import jax
    import jax.numpy as jnp
    def _L0_gnn_ref(A, X, W, b):
        import jax, jax.numpy as jnp
        import numpy as np
        B, N, C, OUT, S = (4, 2048, 256, 256, 25)
        DENSITY = 0.008
        mask = A != 0
        neg_inf = jnp.float32(-jnp.inf)
        pri = -jnp.arange(N, dtype=jnp.float32)
        scores = jnp.where(mask, pri, neg_inf)
        vals, idx = jax.lax.top_k(scores, S)
        valid = vals > neg_inf
        feats = jax.vmap(lambda x, i: x[i])(X, idx)
        feats = jnp.where(valid[..., None], feats, neg_inf)
        agg = feats.max(axis=2)
        degree = mask.sum(axis=-1)
        agg = jnp.where((degree <= S)[..., None], jnp.maximum(agg, 0.0), agg)
        h = jnp.concatenate([X, agg], axis=-1)
        out = jax.nn.relu(jnp.einsum('bnf,fo->bno', h, W) + b)
        return out

    def _L1_gnn_ref(x, adj, edge_types, W, a1, a2, edge_emb, ln_gamma, ln_beta):
        import jax, jax.numpy as jnp
        import numpy as np
        B, N, IN_F, OUT_F, H, NUM_EDGE_TYPES = (16, 512, 256, 256, 8, 50)
        HEAD_DIM = OUT_F // H
        LN_EPS = 1e-05
        Bx, Nx, _ = x.shape
        Wh = (x @ W).reshape(Bx, Nx, H, HEAD_DIM)
        s1 = jnp.einsum('bnhd,d->bnh', Wh, a1)
        s2 = jnp.einsum('bnhd,d->bnh', Wh, a2)
        e = s1[:, :, None, :] + s2[:, None, :, :] + edge_emb[edge_types]
        e = jnp.where(e > 0, e, 0.2 * e)
        e = jnp.where((adj == 0)[..., None], jnp.float32(-1000000000.0), e)
        alpha = jax.nn.softmax(e, axis=2)
        h = jnp.einsum('bijh,bjhd->bihd', alpha, Wh).reshape(Bx, Nx, OUT_F)
        mu = jnp.mean(h, axis=-1, keepdims=True)
        var = jnp.mean(jnp.square(h - mu), axis=-1, keepdims=True)
        hn = (h - mu) * jax.lax.rsqrt(var + LN_EPS) * ln_gamma + ln_beta
        return jax.nn.elu(hn)

    x = _layernorm(x + _L0_gnn_ref(adj, x, L0_gnn_W, L0_gnn_b), axis=-1)
    x = _layernorm(x + _L1_gnn_ref(x, adj, adj, L1_gnn_W, L1_gnn_a1, L1_gnn_a2, L1_gnn_edge_emb, L1_gnn_ln_gamma, L1_gnn_ln_beta), axis=-1)
    return x


_drawn_inputs = setup_inputs


def setup_inputs(seed=0):
    import zlib

    import numpy as np

    out = dict(_drawn_inputs(seed))
    spreads = {'L0_gnn_b': (0.0, 0.1), 'L1_gnn_ln_gamma': (1.0, 0.2), 'L1_gnn_ln_beta': (0.0, 0.1)}
    factors = {'L1_gnn_edge_emb': 8.0}
    for name, (base, spread) in spreads.items():
        noise = np.random.default_rng([zlib.crc32(name.encode()), seed]).standard_normal(out[name].shape)
        drawn = base * np.exp(spread * noise) if base else spread * noise
        out[name] = jnp.asarray(drawn.astype(out[name].dtype))
    for name, factor in factors.items():
        out[name] = (out[name] * factor).astype(out[name].dtype)
    return out
```

```python
import numpy as np
import concourse.bass as bass
from concourse import mybir
from contextlib import ExitStack

F32 = mybir.dt.float32
BF16 = mybir.dt.bfloat16
I32 = mybir.dt.int32
ALU = mybir.AluOpType
ACT = mybir.ActivationFunctionType
AX = mybir.AxisListType.X

P = 128
B, N, C = 8, 2048, 256
H, DH = 8, 32
T = N // P
TOP = 25
LIST = 32
CH = N // 16
CAND = 16 * 8
ROW = C + H
MARK = 4096.0
FAR = -1.0e30
LOWEST = -3.0e38
EPS = 1e-5
SLOTS = [25, 19, 17, 15, 14, 13, 13, 12, 12, 11, 11, 10, 10, 9, 8, 8]
SEARCH = [2, 2, 2, 2, 1, 1, 1, 1, 1, 1, 1, 1, 0, 0, 0, 0]
FINISH = [0, 1, 1, 1, 1, 1, 1, 1, 1, 1, 1, 1, 1, 1, 1, 2]
CONSTS = 22 + T
SORT_AT = 12
LATE_AT = 4


def build(nc, x, adj, w0, b0, w1, a1, a2, emb, gamma, beta, out):
    ctx = ExitStack()
    with ctx:
        def sb(name, shape, dt=F32):
            return ctx.enter_context(nc.sbuf_tensor(name, shape, dt))

        def pb(name, shape):
            return ctx.enter_context(nc.psum_tensor(name, shape, F32))

        def sem(name):
            return ctx.enter_context(nc.semaphore(name))

        def dram(name, width):
            return nc.dram_tensor(name, (B * N, width), F32).ap()

        agg_d = dram("agg_d", C)
        x1_d = dram("x1_d", C)
        table_d = dram("table_d", ROW)
        att_d = dram("att_d", C)

        x_rows = x.rearrange("b n c -> (b n) c")
        adj_rows = adj.rearrange("b n m -> (b n) m")
        out_rows = out.rearrange("b n c -> (b n) c")

        adj_i = [sb(f"adj_i{q}", [P, N], I32) for q in range(2)]
        adj_h2 = sb("adj_h2", [P, 2 * N], BF16)
        adj_h = [adj_h2[:, N * q:N * (q + 1)] for q in range(2)]
        cand = sb("cand", [P, CAND])
        lists = sb("lists", [P, T * LIST])
        eighth = sb("eighth", [P, T])
        degree = sb("degree", [P, B * T])
        key = sb("key", [P, T])
        key2 = sb("key2", [P, T])
        order = sb("order", [P, T])
        picks = sb("picks", [P, B * T * T])
        wide = sb("wide", [P, T * LIST * T])
        moved = sb("moved", [P, T * LIST])
        fill = sb("fill", [P, T * LIST])
        small = sb("small", [P, T * T])
        tile_of = sb("tile_of", [P, T])
        own = sb("own", [P, T])
        idx_all = sb("idx_all", [P, B * T * LIST], I32)
        own_all = sb("own_all", [P, B * T], I32)
        deg_all = sb("deg_all", [P, B * T])
        low_all = sb("low_all", [P, B * T])
        has_all = sb("has_all", [P, B * T])
        hasnt_all = sb("hasnt_all", [P, B * T])
        idx_cur = sb("idx_cur", [P, T * LIST], I32)
        own_cur = sb("own_cur", [P, T], I32)
        flag_in = sb("flag_in", [P, 2])
        flag_i = sb("flag_i", [1, 2 * B], I32)
        rows_g = [sb(f"rows_g{q}", [P, TOP * ROW]) for q in range(2)]
        res = [sb(f"res{q}", [P, C]) for q in range(2)]
        pair = [sb(f"pair{q}", [P, 2 * C]) for q in range(2)]
        h_t = sb("h_t", [P, 2 * C])
        y = sb("y", [P, C])
        z = sb("z", [P, C])
        stats = sb("stats", [P, 12])
        mv = sb("mv", [P, 4])
        var = sb("var", [P, 2])
        std = sb("std", [P, 2])
        rstd = sb("rstd", [P, 2])
        y2 = sb("y2", [P, C])
        x1 = [sb(f"x1{q}", [P, C]) for q in range(2)]
        x1_t = sb("x1_t", [P, C])
        tab = [sb(f"tab{q}", [P, ROW]) for q in range(2)]
        self_s = sb("self_s", [P, B * T * H])
        mean_wh = sb("mean_wh", [P, B * C])
        self_cur = sb("self_cur", [P, T * H])
        far_cur = sb("far_cur", [P, T * LIST])
        e = sb("e", [P, LIST * H])
        pr = sb("pr", [P, LIST * H])
        mx = sb("mx", [P, H])
        su = sb("su", [P, H])
        neg = sb("neg", [P, C])
        w0_s = sb("w0_s", [P, 4, C])
        w1_s = sb("w1_s", [P, 2, ROW + H])
        b0_s = sb("b0_s", [1, C])
        b1_s = sb("b1_s", [1, ROW + H])
        a1_s = sb("a1_s", [P, DH])
        a2_s = sb("a2_s", [P, DH])
        gam = sb("gam", [P, C])
        bet = sb("bet", [P, C])
        ident = sb("ident", [P, P])
        mark_h = sb("mark_h", [P, P], BF16)
        ones_h = sb("ones_h", [64, P], BF16)
        value_row = sb("value_row", [P, N])
        cols_h = sb("cols_h", [64, N], BF16)
        ones = sb("ones", [P, P])
        c_i = sb("c_i", [P, 64], I32)
        rev = sb("rev", [P, T])
        tno = sb("tno", [P, T])
        kno = sb("kno", [P, LIST])
        row_p = sb("row_p", [P, 1])
        base_b = sb("base_b", [P, B])
        slots_c = sb("slots_c", [P, T])
        all_idx = sb("all_idx", [P, LIST], I32)
        all_own = sb("all_own", [P, 1], I32)
        all_res = sb("all_res", [P, C])
        top = sb("top", [P, LIST])
        sums = sb("sums", [P, H])
        lone = sb("lone", [P, 2])
        peak = sb("peak", [P, 1])
        cols_i = wide[:, N:2 * N].bitcast(I32)
        all_g = wide[:, 0:TOP * C]
        mask = adj_i[1][:, :].bitcast(F32)
        heat = adj_h2[:, :].bitcast(F32)
        graph_tab = wide[:, 0:T * ROW]
        heat_t = wide[:, T * ROW:T * ROW + N]

        score_p = [pb(f"score_p{h}", [P, N // 2]) for h in range(2)]
        turn_p = pb("turn_p", [P, 2 * C])
        lin_p = pb("lin_p", [P, 2 * C])
        wh_p = pb("wh_p", [P, 2 * C])
        sum_p = pb("sum_p", [P, 2 * C])

        passed = sem("passed")
        weights_ld = sem("weights_ld")
        consts_done = sem("consts_done")
        weights_done = sem("weights_done")
        adj_ld = [sem(f"adj_ld{q}") for q in range(2)]
        cast_done = sem("cast_done")
        score_ready = sem("score_ready")
        score_used = sem("score_used")
        flag_put = sem("flag_put")
        flag_summed = sem("flag_summed")
        flag_ready = sem("flag_ready")
        again_dma = sem("again_dma")
        again_ld = sem("again_ld")
        again_used = sem("again_used")
        early_ready = sem("early_ready")
        late_ready = sem("late_ready")
        rows_ld = [sem(f"rows_ld{q}") for q in range(2)]
        rows_used = sem("rows_used")
        res_ready = sem("res_ready")
        res_out = [sem(f"res_out{q}") for q in range(2)]
        graph_out = sem("graph_out")
        redo_idx = sem("redo_idx")
        redo_dma = sem("redo_dma")
        redo_ld = sem("redo_ld")
        redo_res = sem("redo_res")
        redo_out = sem("redo_out")
        dense_go = sem("dense_go")
        dense_dma = sem("dense_dma")
        dense_tab = sem("dense_tab")
        dense_adj = sem("dense_adj")
        dense_mask = sem("dense_mask")
        dense_row = sem("dense_row")
        dense_e = sem("dense_e")
        dense_p = sem("dense_p")
        dense_turn = sem("dense_turn")
        dense_pt = sem("dense_pt")
        dense_att = sem("dense_att")
        dense_res = sem("dense_res")
        dense_out = sem("dense_out")
        pair_ld = [sem(f"pair_ld{q}") for q in range(2)]
        turned = sem("turned")
        h_ready = sem("h_ready")
        lin_ready = sem("lin_ready")
        var_ready = sem("var_ready")
        std_ready = sem("std_ready")
        x1_ready = sem("x1_ready")
        x1_turned = sem("x1_turned")
        x1t_ready = sem("x1t_ready")
        wh_ready = sem("wh_ready")
        tab_ready = sem("tab_ready")
        summed = sem("summed")
        mean_ready = sem("mean_ready")
        tab_out = [sem(f"tab_out{q}") for q in range(2)]
        table_ready = sem("table_ready")
        logits_ready = sem("logits_ready")
        exp_ready = sem("exp_ready")
        norm_ready = sem("norm_ready")
        elu_ready = sem("elu_ready")
        pair_used = sem("pair_used")
        final_ready = sem("final_ready")
        final_out = [sem(f"final_out{q}") for q in range(2)]

        def need(eng, s, value):
            if not isinstance(value, int) or value > 0:
                eng.wait_ge(s, value)

        def hold(eng, s, value):
            if not isinstance(value, int):
                eng.wait_ge(s, value)
                eng.sem_inc(passed, 1)
            elif value > 0:
                eng.wait_ge(s, value)

        half, hl = T // 2, T // 2 * LIST

        def landed(eng, dma_sem, count, to):
            eng.wait_ge(dma_sem, count)
            eng.sem_clear(dma_sem)
            eng.sem_inc(to, 1)

        def upto(u):
            return sum(SLOTS[u % 2:u + 1:2])

        def two_back(n, t):
            return n - 1 if t else n

        def tile_rows(b, t):
            return bass.ds(b * N + t * P, P)

        def program(eng, stage1, stage2):
            stage1(-1, True, False, False)
            stage1(0, True, True, False)
            with eng.Fori(1, B - 1) as b:
                stage1(b, True, True, True)
            stage1(B - 1, False, True, True)
            stage1(B, False, False, True)
            stage2(0, True, False)
            with eng.Fori(1, B - 1) as b:
                stage2(b, True, True)
            stage2(B - 1, True, True)
            stage2(B, False, True)

        block = ctx.enter_context(nc.Block())

        @block.sync
        def _(sp):
            sp.dma_start(w0_s[:, :, :], w0.rearrange("(c p) n -> p c n", p=P)).then_inc(weights_ld, 16)
            sp.dma_start(w1_s[:, :, 0:C], w1.rearrange("(c p) n -> p c n", p=P)).then_inc(weights_ld, 16)
            sp.dma_start(b0_s[:, :], b0.rearrange("(a n) -> a n", a=1)).then_inc(weights_ld, 16)
            sp.dma_start(a1_s[:, :], a1.rearrange("(a n) -> a n", a=1).broadcast_to([P, DH])).then_inc(weights_ld, 16)
            sp.dma_start(a2_s[:, :], a2.rearrange("(a n) -> a n", a=1).broadcast_to([P, DH])).then_inc(weights_ld, 16)
            sp.dma_start(gam[:, :], gamma.rearrange("(a n) -> a n", a=1).broadcast_to([P, C])).then_inc(weights_ld, 16)
            sp.dma_start(bet[:, :], beta.rearrange("(a n) -> a n", a=1).broadcast_to([P, C])).then_inc(weights_ld, 16)
            sp.wait_ge(consts_done, 1)
            sp.dma_start(b1_s[:, ROW:ROW + H], emb[1:2, :]).then_inc(weights_ld, 16)

            def load_adj(b, t):
                n, q = b * T + t, t % 2
                need(sp, cast_done, n - 1)
                sp.dma_start(adj_i[q][:, :], adj_rows[tile_rows(b, t), :]).then_inc(adj_ld[q], 16)

            def search_again(b):
                hold(sp, flag_ready, 2 * b + 1)
                over = sp.value_load(flag_i[0:1, bass.ds(2 * b, 1)])
                with sp.If(over > 0):
                    with sp.Fori(0, T) as t:
                        sp.wait_ge(again_used, b * T + t)
                        sp.dma_start(adj_i[0][:, :], adj_rows[bass.ds(b * N + t * P, P), :])\
                            .then_inc(again_dma, 16)
                        landed(sp, again_dma, 16, again_ld)
                with sp.Else():
                    sp.sem_inc(again_ld, T)
                hold(sp, again_used, T * (b + 1))

            def load_pair(b, t):
                n, q = b * T + t, t % 2
                if t == 0:
                    hold(sp, graph_out, b + 1)
                need(sp, x1_ready, two_back(n, t))
                sp.dma_start(pair[q][:, 0:C], x_rows[tile_rows(b, t), :]).then_inc(pair_ld[q], 16)
                sp.dma_start(pair[q][:, C:2 * C], agg_d[tile_rows(b, t), :]).then_inc(pair_ld[q], 16)

            def store_table(b, t):
                n, q = b * T + t, t % 2
                sp.wait_ge(tab_ready, n + 1)
                sp.dma_start(x1_d[tile_rows(b, t), :], x1[q][:, :]).then_inc(tab_out[q], 16)
                sp.dma_start(table_d[tile_rows(b, t), :], tab[q][:, :]).then_inc(tab_out[q], 16)
                if t == T - 1:
                    for q in range(2):
                        sp.wait_ge(tab_out[q], 16 * T * (b + 1))
                    sp.sem_inc(table_ready, 1)

            def stage1(b, search, reduce, finish):
                t_s = t_f = 0
                for u in range(T):
                    for _ in range(SEARCH[u] if search else 0):
                        load_adj(b + 1, t_s)
                        t_s += 1
                    if search and u == SORT_AT:
                        search_again(b + 1)
                    for _ in range(FINISH[u] if finish else 0):
                        if t_f:
                            store_table(b - 1, t_f - 1)
                        load_pair(b - 1, t_f)
                        t_f += 1
                if finish:
                    store_table(b - 1, T - 1)

            def dense(b):
                hold(sp, graph_out, B + b + 1)
                hold(sp, dense_go, b + 1)
                hold(sp, flag_ready, 2 * b + 2)
                many = sp.value_load(flag_i[0:1, bass.ds(2 * b + 1, 1)])
                with sp.If(many > 0):
                    sp.dma_start(graph_tab.rearrange("p (t c) -> p t c", c=ROW),
                                 table_d[bass.ds(b * N, N), :].rearrange("(t p) c -> p t c", p=P))\
                        .then_inc(dense_dma, 16)
                    landed(sp, dense_dma, 16, dense_tab)
                    with sp.Fori(0, T) as t:
                        sp.wait_ge(dense_mask, b * T + t)
                        sp.dma_start(adj_i[0][:, :], adj_rows[bass.ds(b * N + t * P, P), :])\
                            .then_inc(dense_dma, 16)
                        landed(sp, dense_dma, 16, dense_adj)
                        sp.wait_ge(dense_res, b * T + t + 1)
                        sp.dma_start(att_d[bass.ds(b * N + t * P, P), :], all_res[:, :])\
                            .then_inc(dense_dma, 16)
                        landed(sp, dense_dma, 16, dense_out)
                with sp.Else():
                    sp.sem_inc(dense_tab, 1)
                    sp.sem_inc(dense_adj, T)
                    sp.sem_inc(dense_out, T)

            def load_pair2(b, t):
                n, q = b * T + t, t % 2
                if t == 0:
                    hold(sp, graph_out, B + b + 1)
                need(sp, pair_used, two_back(n, t))
                sp.dma_start(pair[q][:, 0:C], att_d[tile_rows(b, t), :]).then_inc(pair_ld[q], 16)
                sp.dma_start(pair[q][:, C:2 * C], x1_d[tile_rows(b, t), :]).then_inc(pair_ld[q], 16)

            def store_final(b, t):
                n, q = b * T + t, t % 2
                sp.wait_ge(final_ready, n + 1)
                sp.dma_start(out_rows[tile_rows(b, t), :], x1[q][:, :]).then_inc(final_out[q], 16)

            def stage2(b, reduce, finish):
                t_f = 0
                for u in range(T):
                    for _ in range(FINISH[u] if finish else 0):
                        if not t_f:
                            dense(b - 1)
                            load_pair2(b - 1, 0)
                        if t_f < T - 1:
                            load_pair2(b - 1, t_f + 1)
                        if t_f:
                            store_final(b - 1, t_f - 1)
                        t_f += 1
                if finish:
                    store_final(b - 1, T - 1)

            program(sp, stage1, stage2)
            for q in range(2):
                sp.wait_ge(final_out[q], 16 * B * T // 2)

        @block.gpsimd
        def _(pool):
            steps = 0

            def step(last):
                nonlocal steps
                steps += 1
                last.then_inc(consts_done, 1)
                pool.wait_ge(consts_done, steps)

            step(pool.memset(b1_s[:, :], 0.0))
            step(pool.memset(ident[:, :], 0.0))
            step(pool.memset(ones[:, :], 1.0))
            step(pool.memset(mark_h[:, :], 0.0))
            step(pool.memset(ones_h[:, :], 1.0))
            step(pool.memset(cols_i[:, :], 0))
            for u in range(T):
                step(pool.memset(slots_c[:, u:u + 1], float(SLOTS[u])))
            step(pool.iota(c_i[:, 0:T], pattern=[[1, T]], base=0, channel_multiplier=0))
            step(pool.iota(c_i[:, T:T + LIST], pattern=[[1, LIST]], base=0, channel_multiplier=0))
            step(pool.iota(c_i[:, 48:49], pattern=[[0, 1]], base=0, channel_multiplier=1))
            step(pool.iota(c_i[:, 49:49 + B], pattern=[[N, B]], base=0, channel_multiplier=0))
            step(pool.iota(cols_i[0:1, :], pattern=[[-8, N // 8], [0, 8]], base=N, channel_multiplier=0))
            step(pool.iota(cols_i[32:33, :], pattern=[[0, N // 8], [-1, 8]], base=0, channel_multiplier=0))
            step(pool.affine_select(out=ident[:, :], in_=ident[:, :], compare_op=ALU.not_equal,
                                    fill=1.0, base=0, pattern=[[-1, P]], channel_multiplier=1))
            step(pool.affine_select(out=mark_h[:, :], in_=mark_h[:, :], compare_op=ALU.not_equal,
                                    fill=MARK, base=0, pattern=[[-1, P]], channel_multiplier=1))
            step(pool.tensor_copy(tno[:, :], c_i[:, 0:T]))
            step(pool.tensor_copy(kno[:, :], c_i[:, T:T + LIST]))
            step(pool.tensor_copy(row_p[:, :], c_i[:, 48:49]))
            step(pool.tensor_copy(base_b[:, :], c_i[:, 49:49 + B]))
            step(pool.tensor_copy(cols_h[:, :], cols_i[0:64, :]))
            step(pool.iota(cols_i[:, :], pattern=[[-1, N]], base=int(MARK) + N, channel_multiplier=0))
            step(pool.tensor_copy(value_row[:, :], cols_i[:, :]))
            step(pool.tensor_scalar(rev[:, :], tno[:, :], -1.0, float(T - 1), ALU.mult, ALU.add))
            assert steps == CONSTS

            redone = pool.alloc_register("redone")
            pool.reg_mov(redone, 0)

            def gather(b, u, table, width, order_b):
                n, q = order_b * T + u, u % 2
                hold(pool, rows_used, n - 1)
                for k in range(SLOTS[u]):
                    at = u * LIST + k
                    pool.indirect_dma_start(
                        out=rows_g[q][:, k * width:(k + 1) * width], out_offset=None, in_=table,
                        in_offset=bass.IndirectOffsetOnAxis(ap=idx_cur[:, at:at + 1], axis=0),
                        bounds_check=B * N - 1, oob_is_err=False).then_inc(rows_ld[q], 16)

            def scatter(order_b, u, to):
                n, q = order_b * T + u, u % 2
                hold(pool, res_ready, n + 1)
                pool.indirect_dma_start(
                    out=to, out_offset=bass.IndirectOffsetOnAxis(ap=own_cur[:, u:u + 1], axis=0),
                    in_=res[q][:, :], in_offset=None, bounds_check=B * N - 1,
                    oob_is_err=False).then_inc(res_out[q], 16)

            def redo(b):
                hold(pool, flag_ready, 2 * b + 2)
                many = pool.value_load(flag_i[0:1, bass.ds(2 * b + 1, 1)])
                with pool.If(many > 0):
                    for q in range(2):
                        hold(pool, res_out[q], 16 * half * (b + 1))
                    with pool.Fori(0, T) as u:
                        hold(pool, redo_idx, b * T + u + 1)
                        for k in range(TOP):
                            pool.indirect_dma_start(
                                out=all_g[:, k * C:(k + 1) * C], out_offset=None, in_=x_rows,
                                in_offset=bass.IndirectOffsetOnAxis(ap=all_idx[:, k:k + 1], axis=0),
                                bounds_check=B * N - 1, oob_is_err=False).then_inc(redo_dma, 16)
                        pool.reg_add(redone, redone, 16 * TOP)
                        pool.wait_ge(redo_dma, redone)
                        pool.sem_inc(redo_ld, 1)
                        hold(pool, redo_res, b * T + u + 1)
                        pool.indirect_dma_start(
                            out=agg_d, out_offset=bass.IndirectOffsetOnAxis(ap=all_own[:, :], axis=0),
                            in_=all_res[:, :], in_offset=None, bounds_check=B * N - 1,
                            oob_is_err=False).then_inc(redo_dma, 16)
                        pool.reg_add(redone, redone, 16)
                        pool.wait_ge(redo_dma, redone)
                        pool.sem_inc(redo_out, 1)
                with pool.Else():
                    pool.sem_inc(redo_ld, T)
                    pool.sem_inc(redo_out, T)

            def end_graph(order_b):
                for q in range(2):
                    hold(pool, res_out[q], 16 * (T // 2) * (order_b + 1))
                pool.sem_inc(graph_out, 1)

            def stage1(b, search, reduce, finish):
                for u in range(T if reduce else 0):
                    if u == 0:
                        hold(pool, early_ready, b + 1)
                    if u == T // 2:
                        hold(pool, late_ready, b + 1)
                    gather(b, u, x_rows, C, b)
                    if u == 0 and finish:
                        scatter(b - 1, T - 1, agg_d)
                        redo(b - 1)
                        end_graph(b - 1)
                    if u:
                        scatter(b, u - 1, agg_d)
                if finish and not reduce:
                    scatter(b - 1, T - 1, agg_d)
                    redo(b - 1)
                    end_graph(b - 1)

            def stage2(b, reduce, finish):
                for u in range(T if reduce else 0):
                    if u == 0:
                        hold(pool, early_ready, B + b + 1)
                        pool.wait_ge(table_ready, B)
                    if u == T // 2:
                        hold(pool, late_ready, B + b + 1)
                    gather(b, u, table_d, ROW, B + b)
                    if u == 0 and finish:
                        scatter(B + b - 1, T - 1, att_d)
                        end_graph(B + b - 1)
                    if u:
                        scatter(B + b, u - 1, att_d)
                if finish and not reduce:
                    scatter(B + b - 1, T - 1, att_d)
                    end_graph(B + b - 1)

            program(pool, stage1, stage2)

        @block.scalar
        def _(act):
            def cast(b, t):
                n, q = b * T + t, t % 2
                act.wait_ge(adj_ld[q], 16 * (b * (T // 2) + t // 2 + 1))
                need(act, score_ready, 2 * n - 2)
                act.activation(adj_h[q], adj_i[q][:, :], ACT.Copy,
                               accum_out=degree[:, bass.ds(n, 1)]).then_inc(cast_done, 1)

            def finish_a(b, t):
                n = b * T + t
                act.wait_ge(turned, n + 1)
                need(act, lin_ready, n)
                act.activation(h_t[:, :], turn_p[:, :], ACT.Copy).then_inc(h_ready, 1)
                act.wait_ge(var_ready, n + 1)
                act.activation(std[:, 0:1], var[:, 0:1], ACT.Sqrt).then_inc(std_ready, 1)

            def finish_b(b, t):
                n, q = b * T + t, t % 2
                act.wait_ge(x1_turned, n + 1)
                need(act, wh_ready, n)
                act.activation(x1_t[:, :], lin_p[:, C:2 * C], ACT.Copy).then_inc(x1t_ready, 1)
                act.wait_ge(wh_ready, n + 1)
                need(act, tab_out[q], 16 * (b * T + t // 2 * 2))
                need(act, summed, two_back(n, t))
                act.activation(tab[q][:, :], wh_p[:, 0:ROW], ACT.Copy)
                act.activation(self_s[:, bass.ds(n * H, H)], wh_p[:, ROW:ROW + H], ACT.Copy)\
                    .then_inc(tab_ready, 1)
                if t == T - 1:
                    act.wait_ge(summed, n + 1)
                    act.activation(mean_wh[:, bass.ds(b * C, C)], sum_p[:, 0:C], ACT.Copy,
                                   scale=1.0 / N).then_inc(mean_ready, 1)

            def stage1(b, search, reduce, finish):
                t_s = t_f = 0
                for u in range(T):
                    for _ in range(SEARCH[u] if search else 0):
                        cast(b + 1, t_s)
                        t_s += 1
                    for _ in range(FINISH[u] if finish else 0):
                        if t_f:
                            finish_b(b - 1, t_f - 1)
                        finish_a(b - 1, t_f)
                        t_f += 1
                if finish:
                    finish_b(b - 1, T - 1)

            def exps(b, u):
                n, w = b * T + u, SLOTS[u] * H
                act.wait_ge(logits_ready, n + 1)
                act.activation(pr[:, 0:w], e[:, 0:w], ACT.Exp).then_inc(exp_ready, 1)

            def elu(b, t):
                n = b * T + t
                act.wait_ge(norm_ready, n + 1)
                act.activation(neg[:, :], z[:, :], ACT.Relu, scale=-1.0)
                act.drain()
                act.activation(neg[:, :], neg[:, :], ACT.Exp, scale=-1.0).then_inc(elu_ready, 1)

            def root(b, j):
                act.wait_ge(var_ready, B * T + b * (T + 1) + j + 1)
                act.activation(std[:, :], var[:, :], ACT.Sqrt).then_inc(std_ready, 1)

            def dense(b):
                hold(act, dense_out, T * b)
                act.wait_ge(flag_ready, 2 * b + 2)
                many = act.value_load(flag_i[0:1, bass.ds(2 * b + 1, 1)])
                with act.If(many > 0):
                    with act.Fori(0, T) as t:
                        with act.Fori(0, H) as h:
                            m = (b * T + t) * H + h
                            act.wait_ge(dense_res, b * T + t)
                            act.wait_ge(dense_e, m + 1)
                            act.activation(heat, heat, ACT.Exp, bias=peak[:, 0:1],
                                           accum_out=sums[:, bass.ds(h, 1)]).then_inc(dense_p, 1)
                            act.wait_ge(dense_att, m)
                            for g in range(4):
                                act.wait_ge(dense_turn, 4 * m + g + 1)
                                act.activation(heat_t[:, 512 * g:512 * (g + 1)], turn_p[:, :],
                                               ACT.Copy).then_inc(dense_pt, 1)
                with act.Else():
                    act.sem_inc(dense_p, T * H)
                    act.sem_inc(dense_pt, 4 * T * H)

            def stage2(b, reduce, finish):
                t_f = 0
                for u in range(T):
                    if reduce:
                        exps(b, u)
                    if u == 0 and finish:
                        dense(b - 1)
                    for _ in range(FINISH[u] if finish else 0):
                        if not t_f:
                            root(b - 1, 0)
                        elu(b - 1, t_f)
                        t_f += 1
                        root(b - 1, t_f)

            program(act, stage1, stage2)

        @block.tensor
        def _(pe):
            pe.wait_ge(consts_done, CONSTS)
            pe.wait_ge(weights_ld, 16 * 8)
            pe.wait_ge(weights_done, 1)

            def scores(b, t):
                n, q = b * T + t, t % 2
                pe.wait_ge(cast_done, n + 1)
                for h in range(2):
                    need(pe, score_used, 2 * n + h - 1)
                    for c in range(2):
                        o = score_p[h][:, 512 * c:512 * (c + 1)]
                        at = slice(1024 * h + 512 * c, 1024 * h + 512 * (c + 1))
                        pe.matmul(o, mark_h[:, :], adj_h[q][:, at], start=True, stop=False)
                        last = pe.matmul(o, ones_h[:, :], cols_h[:, at], start=False, stop=True)
                    last.then_inc(score_ready, 1)

            def sum_flag(k, col):
                pe.wait_ge(flag_put, k)
                pe.matmul(wh_p[0:1, 2 * C - 2 + col:2 * C - 1 + col], ones[:, 0:1],
                          flag_in[:, col:col + 1], start=True, stop=True).then_inc(flag_summed, 1)
                pe.wait_ge(flag_ready, k)

            def finish_a(b, t):
                n, q = b * T + t, t % 2
                pe.wait_ge(pair_ld[q], 16 * (b * T + t // 2 * 2 + 2))
                need(pe, h_ready, n)
                for c in range(4):
                    last = pe.transpose(turn_p[:, P * c:P * (c + 1)], pair[q][:, P * c:P * (c + 1)],
                                        ident[:, :])
                last.then_inc(turned, 1)
                pe.wait_ge(h_ready, n + 1)
                need(pe, x1_ready, n)
                pe.matmul(lin_p[:, 0:C], ones[0:1, :], b0_s[0:1, :], start=True, stop=False)
                for c in range(4):
                    last = pe.matmul(lin_p[:, 0:C], h_t[:, P * c:P * (c + 1)], w0_s[:, c, :],
                                     start=False, stop=(c == 3))
                last.then_inc(lin_ready, 1)

            def finish_b(b, t):
                n, q = b * T + t, t % 2
                pe.wait_ge(x1_ready, n + 1)
                need(pe, x1t_ready, n)
                for c in range(2):
                    last = pe.transpose(lin_p[:, C + P * c:C + P * (c + 1)],
                                        x1[q][:, P * c:P * (c + 1)], ident[:, :])
                last.then_inc(x1_turned, 1)
                pe.wait_ge(x1t_ready, n + 1)
                need(pe, tab_ready, n)
                pe.matmul(wh_p[:, 0:ROW + H], ones[0:1, :], b1_s[0:1, :], start=True, stop=False)
                for c in range(2):
                    last = pe.matmul(wh_p[:, 0:ROW + H], x1_t[:, P * c:P * (c + 1)], w1_s[:, c, :],
                                     start=False, stop=(c == 1))
                last.then_inc(wh_ready, 1)
                pe.wait_ge(tab_ready, n + 1)
                if t == 0:
                    need(pe, mean_ready, b)
                pe.matmul(sum_p[:, 0:C], ones[:, :], tab[q][:, 0:C], start=(t == 0),
                          stop=(t == T - 1)).then_inc(summed, 1)

            def stage1(b, search, reduce, finish):
                t_s = t_f = 0
                for u in range(T):
                    for _ in range(SEARCH[u] if search else 0):
                        scores(b + 1, t_s)
                        t_s += 1
                    if search and u == SORT_AT:
                        sum_flag(2 * b + 3, 0)
                        sum_flag(2 * b + 4, 1)
                    for _ in range(FINISH[u] if finish else 0):
                        if t_f:
                            finish_b(b - 1, t_f - 1)
                        finish_a(b - 1, t_f)
                        t_f += 1
                if finish:
                    finish_b(b - 1, T - 1)

            def dense(b):
                hold(pe, dense_out, T * b)
                pe.wait_ge(flag_ready, 2 * b + 2)
                many = pe.value_load(flag_i[0:1, bass.ds(2 * b + 1, 1)])
                with pe.If(many > 0):
                    hold(pe, dense_tab, b + 1)
                    with pe.Fori(0, T) as t:
                        for h in range(H):
                            m = (b * T + t) * H + h
                            pe.wait_ge(dense_e, m)
                            for c in range(T):
                                last = pe.matmul(
                                    score_p[c // 8][:, P * (c % 8):P * (c % 8 + 1)],
                                    graph_tab[:, c * ROW + C + h:c * ROW + C + h + 1].broadcast_to([P, P]),
                                    ident[:, :], start=True, stop=True)
                            last.then_inc(dense_row, 1)
                            pe.wait_ge(dense_p, m + 1)
                            for g in range(4):
                                pe.wait_ge(dense_pt, 4 * m + g)
                                for c in range(4 * g, 4 * g + 4):
                                    last = pe.transpose(turn_p[:, P * (c % 4):P * (c % 4 + 1)],
                                                        heat[:, P * c:P * (c + 1)], ident[:, :])
                                last.then_inc(dense_turn, 1)
                            pe.wait_ge(dense_pt, 4 * m + 4)
                            pe.wait_ge(dense_res, b * T + t)
                            for c in range(T):
                                last = pe.matmul(sum_p[:, h * DH:(h + 1) * DH],
                                                 heat_t[:, P * c:P * (c + 1)],
                                                 graph_tab[:, c * ROW + h * DH:c * ROW + (h + 1) * DH],
                                                 start=(c == 0), stop=(c == T - 1))
                            last.then_inc(dense_att, 1)
                with pe.Else():
                    pe.sem_inc(dense_row, T * H)
                    pe.sem_inc(dense_turn, 4 * T * H)
                    pe.sem_inc(dense_att, T * H)

            def stage2(b, reduce, finish):
                if finish:
                    dense(b - 1)

            program(pe, stage1, stage2)

        @block.vector
        def _(dve):
            v = nc.vector

            def settle():
                v.drain()

            dve.wait_ge(weights_ld, 16 * 8)
            for a_s, to in ((a2_s, C), (a1_s, ROW)):
                for c in range(2):
                    prod = wide[:, C * c:C * (c + 1)].rearrange("p (h d) -> p h d", d=DH)
                    v.tensor_tensor(prod, w1_s[:, c, 0:C].rearrange("p (h d) -> p h d", d=DH),
                                    a_s[:, :].unsqueeze(1).broadcast_to([P, H, DH]), ALU.mult)
                settle()
                for c in range(2):
                    prod = wide[:, C * c:C * (c + 1)].rearrange("p (h d) -> p h d", d=DH)
                    v.tensor_reduce(w1_s[:, c, to:to + H], prod, AX, ALU.add)
                settle()
            v.drain().then_inc(weights_done, 1)
            dve.wait_ge(consts_done, CONSTS)

            def top_lists(src, put):
                for r in range(4):
                    v.max(put(r), src)
                    settle()
                    if r < 3:
                        v.match_replace(src, put(r), src, 0.0)
                        settle()

            def search(b, t):
                n = b * T + t
                settle()
                for h in range(2):
                    hold(dve, score_ready, 2 * n + h + 1)
                    for c in range(8):
                        at = 8 * (8 * h + c)
                        last = v.max(cand[:, at:at + 8], score_p[h][:, CH * c:CH * (c + 1)])
                    last.then_inc(score_used, 1)
                settle()
                v.tensor_reduce(eighth[:, t:t + 1],
                                cand[:, :].rearrange("p (c k) -> p c k", k=8)[:, :, 7], AX, ALU.max)
                settle()
                top_lists(cand[:, :], lambda r: lists[:, t * LIST + 8 * r:t * LIST + 8 * r + 8])

            def search_again(b):
                settle()
                v.tensor_reduce(flag_in[:, 1:2], eighth[:, :], AX, ALU.max)
                settle()
                v.tensor_scalar(flag_in[:, 0:1], flag_in[:, 1:2], MARK, None, ALU.is_gt)\
                    .then_inc(flag_put, 1)
                hold(dve, flag_summed, 2 * b + 1)
                v.tensor_copy(flag_i[0:1, bass.ds(2 * b, 1)], wh_p[0:1, 2 * C - 2:2 * C - 1])\
                    .then_inc(flag_ready, 1)
                hold(dve, flag_ready, 2 * b + 1)
                over = dve.value_load(flag_i[0:1, bass.ds(2 * b, 1)])
                with dve.If(over > 0):
                    with dve.Fori(0, T) as t:
                        dve.wait_ge(again_ld, b * T + t + 1)
                        v.tensor_tensor(wide[:, 0:N], adj_i[0][:, :], value_row[:, :], ALU.mult)\
                            .then_inc(again_used, 1)
                        settle()
                        top_lists(wide[:, 0:N], lambda r: top[:, 8 * r:8 * r + 8])
                        settle()
                        v.tensor_copy(lists[:, bass.ds(t * LIST, LIST)], top[:, :])
                        settle()
                with dve.Else():
                    dve.sem_inc(again_used, T)

            def sort(b):
                at, cur = bass.ds(b * T, T), bass.ds(b * T * LIST, T * LIST)
                v.scalar_tensor_tensor(key[:, :], degree[:, at], float(T), rev[:, :],
                                       ALU.mult, ALU.add)
                settle()
                v.max(order[:, 0:8], key[:, :])
                settle()
                v.match_replace(key2[:, :], order[:, 0:8], key[:, :], -1.0)
                settle()
                v.max(order[:, 8:16], key2[:, :])
                settle()
                pick = picks[:, bass.ds(b * T * T, T * T)].rearrange("p (u t) -> p u t", t=T)
                v.tensor_tensor(pick, order[:, :].unsqueeze(2).broadcast_to([P, T, T]),
                                key[:, :].unsqueeze(1).broadcast_to([P, T, T]), ALU.is_equal)
                settle()
                prod = wide[:, :].rearrange("p (u k t) -> p u k t", k=LIST, t=T)
                v.tensor_tensor(prod, pick.unsqueeze(2).broadcast_to([P, T, LIST, T]),
                                lists[:, :].rearrange("p (t k) -> p k t", k=LIST).unsqueeze(1)
                                .broadcast_to([P, T, LIST, T]), ALU.mult)
                prod2 = small[:, :].rearrange("p (u t) -> p u t", t=T)
                v.tensor_tensor(prod2, pick, tno[:, :].unsqueeze(1).broadcast_to([P, T, T]), ALU.mult)
                settle()
                v.tensor_reduce(moved[:, :], wide[:, :].rearrange("p (a t) -> p a t", t=T), AX, ALU.add)
                v.tensor_reduce(tile_of[:, :], prod2, AX, ALU.add)
                settle()
                first = moved[:, :].rearrange("p (u k) -> p u k", k=LIST)[:, :, 0:1]\
                    .broadcast_to([P, T, LIST])
                m3 = moved[:, :].rearrange("p (u k) -> p u k", k=LIST)
                v.scalar_tensor_tensor(fill[:, :].rearrange("p (u k) -> p u k", k=LIST), m3, MARK,
                                       first, ALU.is_le, ALU.mult)
                v.tensor_tensor(order[:, :], order[:, :], tile_of[:, :], ALU.add)
                v.tensor_scalar(own[:, :], tile_of[:, :], float(P), row_p[:, 0:1], ALU.mult, ALU.add)
                settle()
                v.scalar_tensor_tensor(moved[:, :], moved[:, :], MARK, moved[:, :],
                                       ALU.is_gt, ALU.mult)
                v.tensor_scalar(deg_all[:, at], order[:, :], float(T - 1), 1.0 / T,
                                ALU.subtract, ALU.mult)
                v.tensor_scalar(own_all[:, at], own[:, :], base_b[:, bass.ds(b, 1)], None, ALU.add)
                settle()
                v.tensor_tensor(moved[:, :], moved[:, :], fill[:, :], ALU.add)
                v.tensor_scalar(low_all[:, at], deg_all[:, at], float(TOP), LOWEST, ALU.is_gt, ALU.mult)
                v.tensor_scalar(has_all[:, at], deg_all[:, at], 0.5, None, ALU.is_gt)
                v.tensor_scalar(hasnt_all[:, at], deg_all[:, at], 0.5, None, ALU.is_lt)
                v.tensor_tensor(key[:, :], deg_all[:, at], slots_c[:, :], ALU.subtract)
                settle()
                v.tensor_scalar(moved[:, :], moved[:, :], -1.0, MARK + N, ALU.mult, ALU.add)
                v.tensor_reduce(key2[:, 0:1], key[:, :], AX, ALU.max)
                settle()
                v.tensor_scalar(idx_all[:, cur], moved[:, :], float(N - 1), base_b[:, bass.ds(b, 1)],
                                ALU.min, ALU.add)
                v.tensor_scalar(flag_in[:, 1:2], key2[:, 0:1], 0.0, None, ALU.is_gt)\
                    .then_inc(flag_put, 1)
                hold(dve, flag_summed, 2 * b + 2)
                v.tensor_copy(flag_i[0:1, bass.ds(2 * b + 1, 1)], wh_p[0:1, 2 * C - 1:2 * C])\
                    .then_inc(flag_ready, 1)

            def early_lists(b, order_b):
                settle()
                hold(dve, rows_ld[1], 16 * ((order_b - 1) * upto(T - 1) + upto(half - 1)))
                hold(dve, res_out[0], 16 * ((order_b - 1) * half + half // 2))
                hold(dve, res_out[1], 16 * ((order_b - 1) * half + half // 2))
                v.tensor_copy(idx_cur[:, 0:hl], idx_all[:, bass.ds(b * T * LIST, hl)])
                v.tensor_copy(own_cur[:, 0:half], own_all[:, bass.ds(b * T, half)]).then_inc(early_ready, 1)

            def late_lists(b, order_b):
                hold(dve, res_out[0], 16 * (order_b * half))
                hold(dve, res_out[1], 16 * (order_b * half))
                v.tensor_copy(idx_cur[:, hl:2 * hl], idx_all[:, bass.ds(b * T * LIST + hl, hl)])
                v.tensor_copy(own_cur[:, half:T], own_all[:, bass.ds(b * T + half, half)])\
                    .then_inc(late_ready, 1)

            def wait_rows(order_b, u):
                q = u % 2
                dve.wait_ge(rows_ld[q], 16 * (order_b * upto(T - 2 + q) + upto(u)))

            def max_tile(b, u):
                n, q, k = b * T + u, u % 2, SLOTS[u]
                settle()
                wait_rows(b, u)
                v.tensor_reduce(y[:, :], rows_g[q][:, 0:k * C].rearrange("p (k c) -> p c k", c=C),
                                AX, ALU.max).then_inc(rows_used, 1)
                hold(dve, res_out[q], 16 * (b * half + u // 2))
                settle()
                v.tensor_scalar(res[q][:, :], y[:, :], low_all[:, bass.ds(n, 1)],
                                has_all[:, bass.ds(n, 1)], ALU.max, ALU.mult).then_inc(res_ready, 1)

            def variance(src, j, last=None):
                v.bn_stats(stats[:, 6 * j:6 * j + 6], src)
                settle()
                v.bn_aggr(mv[:, 2 * j:2 * j + 2], stats[:, 6 * j:6 * j + 6])
                settle()
                return v.tensor_scalar(var[:, j:j + 1], mv[:, 2 * j + 1:2 * j + 2], EPS, None, ALU.add)

            def normal(dst, src, j):
                return v.tensor_scalar(dst, src, mv[:, 2 * j:2 * j + 1], rstd[:, j:j + 1],
                                       ALU.subtract, ALU.mult)

            def finish_a(b, t):
                n, q = b * T + t, t % 2
                settle()
                hold(dve, lin_ready, n + 1)
                v.scalar_tensor_tensor(z[:, :], lin_p[:, 0:C], 0.0, pair[q][:, 0:C], ALU.max, ALU.add)
                settle()
                variance(z[:, :], 0).then_inc(var_ready, 1)

            def finish_b(b, t):
                n, q = b * T + t, t % 2
                dve.wait_ge(std_ready, n + 1)
                v.reciprocal(rstd[:, 0:1], std[:, 0:1])
                hold(dve, tab_out[q], 16 * (b * T + t // 2 * 2))
                settle()
                hold(dve, x1_turned, two_back(n, t))
                normal(x1[q][:, :], z[:, :], 0).then_inc(x1_ready, 1)

            def redo(b):
                settle()
                hold(dve, redo_out, T * b)
                hold(dve, flag_ready, 2 * b + 2)
                many = dve.value_load(flag_i[0:1, bass.ds(2 * b + 1, 1)])
                with dve.If(many > 0):
                    with dve.Fori(0, T) as u:
                        n = b * T + u
                        hold(dve, redo_out, n)
                        v.tensor_copy(all_idx[:, :], idx_all[:, bass.ds(n * LIST, LIST)])
                        v.tensor_copy(all_own[:, :], own_all[:, bass.ds(n, 1)])
                        v.drain().then_inc(redo_idx, 1)
                        hold(dve, redo_ld, n + 1)
                        v.tensor_reduce(y[:, :], all_g.rearrange("p (k c) -> p c k", c=C),
                                        AX, ALU.max)
                        settle()
                        v.tensor_scalar(all_res[:, :], y[:, :], low_all[:, bass.ds(n, 1)],
                                        has_all[:, bass.ds(n, 1)], ALU.max, ALU.mult)
                        v.drain().then_inc(redo_res, 1)
                with dve.Else():
                    dve.sem_inc(redo_idx, T)
                    dve.sem_inc(redo_res, T)
                settle()

            def stage1(b, search_, reduce, finish):
                t_s = t_f = 0
                for u in range(T):
                    for _ in range(SEARCH[u] if search_ else 0):
                        search(b + 1, t_s)
                        t_s += 1
                    if search_ and u == SORT_AT:
                        search_again(b + 1)
                        sort(b + 1)
                    if reduce and u == LATE_AT:
                        late_lists(b, b)
                    f = FINISH[u] if finish else 0
                    if f:
                        finish_a(b - 1, t_f)
                    if reduce:
                        max_tile(b, u)
                    if finish and u == 0:
                        redo(b - 1)
                    for i in range(f):
                        if i:
                            finish_a(b - 1, t_f)
                        finish_b(b - 1, t_f)
                        t_f += 1
                if search_:
                    settle()
                    early_lists(b + 1, b + 1)
                elif reduce:
                    early_lists(0, B)

            def graph_terms(b):
                settle()
                prod = wide[:, 0:T * H * T].rearrange("p (u h t) -> p u h t", h=H, t=T)
                pick = picks[:, bass.ds(b * T * T, T * T)].rearrange("p (u t) -> p u t", t=T)
                v.tensor_tensor(prod, pick.unsqueeze(2).broadcast_to([P, T, H, T]),
                                self_s[:, bass.ds(b * T * H, T * H)]
                                .rearrange("p (t h) -> p h t", h=H).unsqueeze(1)
                                .broadcast_to([P, T, H, T]), ALU.mult)
                v.tensor_tensor(far_cur[:, :].rearrange("p (u k) -> p u k", k=LIST),
                                kno[:, :].unsqueeze(1).broadcast_to([P, T, LIST]),
                                deg_all[:, bass.ds(b * T, T)].unsqueeze(2).broadcast_to([P, T, LIST]),
                                ALU.is_ge)
                settle()
                v.tensor_reduce(self_cur[:, :], wide[:, 0:T * H * T].rearrange("p (a t) -> p a t", t=T),
                                AX, ALU.add)
                v.tensor_scalar(far_cur[:, :], far_cur[:, :], FAR, None, ALU.mult)
                settle()

            def logits(b, u):
                n, q, k = b * T + u, u % 2, SLOTS[u]
                g3 = rows_g[q][:, 0:k * ROW].rearrange("p (k c) -> p k c", c=ROW)
                e3 = e[:, 0:k * H].rearrange("p (k h) -> p k h", h=H)
                settle()
                wait_rows(B + b, u)
                v.tensor_tensor(e3, g3[:, :, C:ROW], self_cur[:, u * H:(u + 1) * H].unsqueeze(1)
                                .broadcast_to([P, k, H]), ALU.add)
                settle()
                v.scalar_tensor_tensor(e[:, 0:k * H], e[:, 0:k * H], 0.2, e[:, 0:k * H],
                                       ALU.mult, ALU.max)
                settle()
                v.tensor_tensor(e3, e3, far_cur[:, u * LIST:u * LIST + k].unsqueeze(2)
                                .broadcast_to([P, k, H]), ALU.add)
                settle()
                v.tensor_reduce(mx[:, :], e3.rearrange("p k h -> p h k"), AX, ALU.max)
                settle()
                v.tensor_tensor(e3, e3, mx[:, :].unsqueeze(1).broadcast_to([P, k, H]), ALU.subtract)\
                    .then_inc(logits_ready, 1)

            def attend(b, u):
                n, q, k = b * T + u, u % 2, SLOTS[u]
                g3 = rows_g[q][:, 0:k * ROW].rearrange("p (k c) -> p k c", c=ROW)
                p3 = pr[:, 0:k * H].rearrange("p (k h) -> p k h", h=H)
                settle()
                dve.wait_ge(exp_ready, n + 1)
                v.tensor_reduce(su[:, :], p3.rearrange("p k h -> p h k"), AX, ALU.add)
                settle()
                v.reciprocal(su[:, :], su[:, :])
                settle()
                v.tensor_scalar(su[:, :], su[:, :], has_all[:, bass.ds(n, 1)], None, ALU.mult)
                settle()
                v.tensor_tensor(p3, p3, su[:, :].unsqueeze(1).broadcast_to([P, k, H]), ALU.mult)
                settle()
                g4 = g3[:, :, 0:C].rearrange("p k (h d) -> p k h d", d=DH)
                v.tensor_tensor(g4, g4, p3.unsqueeze(3).broadcast_to([P, k, H, DH]), ALU.mult)
                settle()
                v.tensor_reduce(y[:, :], g3[:, :, 0:C].rearrange("p k c -> p c k"), AX, ALU.add)\
                    .then_inc(rows_used, 1)
                hold(dve, res_out[q], 16 * ((B + b) * half + u // 2))
                settle()
                v.scalar_tensor_tensor(res[q][:, :], mean_wh[:, bass.ds(b * C, C)],
                                       hasnt_all[:, bass.ds(n, 1)], y[:, :], ALU.mult, ALU.add)\
                    .then_inc(res_ready, 1)

            def wait_pair(b, t):
                hold(dve, pair_ld[t % 2], 16 * (B * T + b * T + t // 2 * 2 + 2))

            def norm_att(b, t):
                n, q = b * T + t, t % 2
                settle()
                dve.wait_ge(std_ready, B * T + b * (T + 1) + t + 1)
                v.reciprocal(rstd[:, :], std[:, :])
                if t:
                    hold(dve, final_out[1 - q], 16 * (b * half + (t - 1) // 2))
                settle()
                if t:
                    normal(x1[1 - q][:, :], y2[:, :], 1).then_inc(final_ready, 1)
                normal(z[:, :], pair[q][:, 0:C], 0)
                settle()
                v.tensor_tensor(z[:, :], z[:, :], gam[:, :], ALU.mult)
                settle()
                v.tensor_tensor(z[:, :], z[:, :], bet[:, :], ALU.add).then_inc(norm_ready, 1)

            def residual(b, t):
                n, q = b * T + t, t % 2
                settle()
                hold(dve, elu_ready, n + 1)
                v.scalar_tensor_tensor(y2[:, :], z[:, :], 0.0, neg[:, :], ALU.max, ALU.add)
                if t < T - 1:
                    wait_pair(b, t + 1)
                settle()
                v.scalar_tensor_tensor(y2[:, :], y2[:, :], -1.0, pair[q][:, C:2 * C], ALU.add, ALU.add)\
                    .then_inc(pair_used, 1)
                if t < T - 1:
                    variance(pair[1 - q][:, 0:C], 0)
                settle()
                variance(y2[:, :], 1)
                v.drain().then_inc(var_ready, 1)

            def last_norm(b):
                hold(dve, std_ready, B * T + (b + 1) * (T + 1))
                settle()
                v.reciprocal(rstd[:, :], std[:, :])
                hold(dve, final_out[1], 16 * (b * half + half - 1))
                settle()
                normal(x1[1][:, :], y2[:, :], 1).then_inc(final_ready, 1)

            def dense(b):
                hold(dve, dense_out, T * b)
                v.drain().then_inc(dense_go, 1)
                hold(dve, flag_ready, 2 * b + 2)
                many = dve.value_load(flag_i[0:1, bass.ds(2 * b + 1, 1)])
                with dve.If(many > 0):
                    with dve.Fori(0, T) as t:
                        n = b * T + t
                        hold(dve, dense_adj, n + 1)
                        hold(dve, dense_turn, 4 * H * n)
                        v.tensor_scalar(mask, adj_i[0][:, :], -FAR, FAR, ALU.mult, ALU.add)\
                            .then_inc(dense_mask, 1)
                        settle()
                        with dve.Fori(0, H) as h:
                            m = n * H + h
                            hold(dve, dense_turn, 4 * m)
                            hold(dve, dense_row, m + 1)
                            for g in range(2):
                                v.tensor_scalar(heat[:, 1024 * g:1024 * (g + 1)], score_p[g][:, :],
                                                self_s[:, bass.ds(m, 1)], None, ALU.add)
                            settle()
                            v.scalar_tensor_tensor(heat, heat, 0.2, heat, ALU.mult, ALU.max)
                            settle()
                            v.tensor_tensor(heat, heat, mask, ALU.add)
                            settle()
                            v.tensor_reduce(peak[:, :], heat, AX, ALU.max)
                            settle()
                            v.tensor_scalar(peak[:, :], peak[:, :], -1.0, None, ALU.mult)
                            v.drain().then_inc(dense_e, 1)
                        v.tensor_scalar(lone[:, 0:1], degree[:, bass.ds(n, 1)], 0.5, None, ALU.is_gt)
                        v.tensor_scalar(lone[:, 1:2], degree[:, bass.ds(n, 1)], 0.5, None, ALU.is_lt)
                        hold(dve, dense_att, H * (n + 1))
                        hold(dve, dense_out, n)
                        v.reciprocal(su[:, :], sums[:, :])
                        settle()
                        v.tensor_scalar(su[:, :], su[:, :], lone[:, 0:1], None, ALU.mult)
                        settle()
                        v.tensor_tensor(y[:, :].rearrange("p (h d) -> p h d", d=DH),
                                        sum_p[:, 0:C].rearrange("p (h d) -> p h d", d=DH),
                                        su[:, :].unsqueeze(2).broadcast_to([P, H, DH]), ALU.mult)
                        settle()
                        v.scalar_tensor_tensor(all_res[:, :], mean_wh[:, bass.ds(b * C, C)],
                                               lone[:, 1:2], y[:, :], ALU.mult, ALU.add)
                        v.drain().then_inc(dense_res, 1)
                with dve.Else():
                    dve.sem_inc(dense_mask, T)
                    dve.sem_inc(dense_e, T * H)
                    dve.sem_inc(dense_res, T)
                settle()

            def stage2(b, reduce, finish):
                t_f = 0
                if reduce:
                    if isinstance(b, int) and b == 0:
                        dve.wait_ge(mean_ready, B)
                        for q in range(2):
                            dve.wait_ge(tab_out[q], 16 * B * T)
                        v.memset(var[:, :], 1.0)
                    graph_terms(b)
                for u in range(T):
                    if reduce and u == LATE_AT:
                        late_lists(b, B + b)
                    if reduce:
                        logits(b, u)
                    f = FINISH[u] if finish else 0
                    if f:
                        if t_f == 0:
                            wait_pair(b - 1, 0)
                            settle()
                            variance(pair[0][:, 0:C], 0)
                            v.drain().then_inc(var_ready, 1)
                        norm_att(b - 1, t_f)
                    if reduce:
                        attend(b, u)
                    if finish and u == 0:
                        dense(b - 1)
                    for i in range(f):
                        if i:
                            norm_att(b - 1, t_f)
                        residual(b - 1, t_f)
                        t_f += 1
                if finish:
                    last_norm(b - 1)
                if reduce and not (isinstance(b, int) and b == B - 1):
                    early_lists(b + 1, B + b + 1)

            program(dve, stage1, stage2)


_INS = ["x", "adj", "L0_gnn_W", "L0_gnn_b", "L1_gnn_W", "L1_gnn_a1", "L1_gnn_a2",
        "L1_gnn_edge_emb", "L1_gnn_ln_gamma", "L1_gnn_ln_beta"]


def kernel(**inputs):
    import numpy as _np
    import concourse.bacc as _bacc
    from concourse import mybir as _mybir
    from concourse.bass_utils import run_bass_kernel_spmd as _run

    nc = _bacc.Bacc("TRN2", target_bir_lowering=False, num_devices=1)
    arrays, args = {}, []
    for name in _INS:
        a = _np.ascontiguousarray(inputs[name])
        arrays[f"in_{name}_dram"] = a
        args.append(nc.dram_tensor(f"in_{name}_dram", a.shape, _mybir.dt.from_np(a.dtype),
                                   kind="ExternalInput").ap())
    out = nc.dram_tensor("out_dram", (B, N, C), _mybir.dt.float32, kind="ExternalOutput").ap()
    build(nc, *args, out)
    r = _run(nc, [arrays], core_ids=[0])
    return r.results[0]["out_dram"]
```

```python
import numpy as np
import concourse.bass as bass
from concourse import mybir
from contextlib import ExitStack

F32 = mybir.dt.float32
BF16 = mybir.dt.bfloat16
I32 = mybir.dt.int32
ALU = mybir.AluOpType
ACT = mybir.ActivationFunctionType
AX = mybir.AxisListType.X

P = 128
B, N, C = 8, 2048, 256
H, DH = 8, 32
T = N // P
TOP = 25
LIST = 32
CH = N // 16
CAND = 16 * 8
ROW = C + H
MARK = 4096.0
FAR = -1.0e30
LOWEST = -3.0e38
EPS = 1e-5
SLOTS = [25, 19, 17, 15, 14, 13, 13, 12, 12, 11, 11, 10, 10, 9, 8, 8]
SEARCH = [2, 2, 2, 2, 1, 1, 1, 1, 1, 1, 1, 1, 0, 0, 0, 0]
FINISH = [0, 1, 1, 1, 1, 1, 1, 1, 1, 1, 1, 1, 1, 1, 1, 2]
CONSTS = 22 + T
SORT_AT = 12
LATE_AT = 4


def build(nc, x, adj, w0, b0, w1, a1, a2, emb, gamma, beta, out):
    ctx = ExitStack()
    with ctx:
        def sb(name, shape, dt=F32):
            return ctx.enter_context(nc.sbuf_tensor(name, shape, dt))

        def pb(name, shape):
            return ctx.enter_context(nc.psum_tensor(name, shape, F32))

        def sem(name):
            return ctx.enter_context(nc.semaphore(name))

        def dram(name, width):
            return nc.dram_tensor(name, (B * N, width), F32).ap()

        agg_d = dram("agg_d", C)
        x1_d = dram("x1_d", C)
        table_d = dram("table_d", ROW)
        first_d = nc.dram_tensor("first_d", (N, ROW), F32).ap()
        att_d = dram("att_d", C)

        x_rows = x.rearrange("b n c -> (b n) c")
        adj_rows = adj.rearrange("b n m -> (b n) m")
        out_rows = out.rearrange("b n c -> (b n) c")

        adj_i = [sb(f"adj_i{q}", [P, N], I32) for q in range(2)]
        adj_h2 = sb("adj_h2", [P, 2 * N], BF16)
        adj_h = [adj_h2[:, N * q:N * (q + 1)] for q in range(2)]
        cand = sb("cand", [P, CAND])
        lists = sb("lists", [P, T * LIST])
        eighth = sb("eighth", [P, T])
        degree = sb("degree", [P, B * T])
        key = sb("key", [P, T])
        key2 = sb("key2", [P, T])
        order = sb("order", [P, T])
        picks = sb("picks", [P, B * T * T])
        wide = sb("wide", [P, T * LIST * T])
        moved = sb("moved", [P, T * LIST])
        fill = sb("fill", [P, T * LIST])
        small = sb("small", [P, T * T])
        tile_of = sb("tile_of", [P, T])
        own = sb("own", [P, T])
        idx_all = sb("idx_all", [P, B * T * LIST], I32)
        own_all = sb("own_all", [P, B * T], I32)
        deg_all = sb("deg_all", [P, B * T])
        low_all = sb("low_all", [P, B * T])
        has_all = sb("has_all", [P, B * T])
        hasnt_all = sb("hasnt_all", [P, B * T])
        idx_cur = sb("idx_cur", [P, T * LIST], I32)
        own_cur = sb("own_cur", [P, T], I32)
        flag_in = sb("flag_in", [P, 2])
        flag_i = sb("flag_i", [1, 2 * B], I32)
        rows_g = [sb(f"rows_g{q}", [P, TOP * ROW]) for q in range(2)]
        res = [sb(f"res{q}", [P, C]) for q in range(2)]
        pair = [sb(f"pair{q}", [P, 2 * C]) for q in range(2)]
        h_t = sb("h_t", [P, 2 * C])
        y = sb("y", [P, C])
        z = sb("z", [P, C])
        stats = sb("stats", [P, 12])
        mv = sb("mv", [P, 4])
        var = sb("var", [P, 2])
        std = sb("std", [P, 2])
        rstd = sb("rstd", [P, 2])
        y2 = sb("y2", [P, C])
        x1 = [sb(f"x1{q}", [P, C]) for q in range(2)]
        x1_t = sb("x1_t", [P, C])
        tab = [sb(f"tab{q}", [P, ROW]) for q in range(2)]
        self_s = sb("self_s", [P, B * T * H])
        mean_wh = sb("mean_wh", [P, B * C])
        self_cur = sb("self_cur", [P, T * H])
        far_cur = sb("far_cur", [P, T * LIST])
        e = sb("e", [P, LIST * H])
        pr = sb("pr", [P, LIST * H])
        mx = sb("mx", [P, H])
        su = sb("su", [P, H])
        neg = sb("neg", [P, C])
        w0_s = sb("w0_s", [P, 4, C])
        w1_s = sb("w1_s", [P, 2, ROW + H])
        b0_s = sb("b0_s", [1, C])
        b1_s = sb("b1_s", [1, ROW + H])
        a1_s = sb("a1_s", [P, DH])
        a2_s = sb("a2_s", [P, DH])
        gam = sb("gam", [P, C])
        bet = sb("bet", [P, C])
        ident = sb("ident", [P, P])
        mark_h = sb("mark_h", [P, P], BF16)
        ones_h = sb("ones_h", [64, P], BF16)
        value_row = sb("value_row", [P, N])
        cols_h = sb("cols_h", [64, N], BF16)
        ones = sb("ones", [P, P])
        c_i = sb("c_i", [P, 64], I32)
        rev = sb("rev", [P, T])
        tno = sb("tno", [P, T])
        kno = sb("kno", [P, LIST])
        row_p = sb("row_p", [P, 1])
        base_b = sb("base_b", [P, B])
        slots_c = sb("slots_c", [P, T])
        all_idx = sb("all_idx", [P, LIST], I32)
        all_own = sb("all_own", [P, 1], I32)
        all_res = sb("all_res", [P, C])
        top = sb("top", [P, LIST])
        sums = sb("sums", [P, H])
        lone = sb("lone", [P, 2])
        peak = sb("peak", [P, 1])
        cols_i = wide[:, N:2 * N].bitcast(I32)
        all_g = wide[:, 0:TOP * C]
        mask = adj_i[1][:, :].bitcast(F32)
        heat = adj_h2[:, :].bitcast(F32)
        graph_tab = wide[:, 0:T * ROW]
        heat_t = wide[:, T * ROW:T * ROW + N]

        score_p = [pb(f"score_p{h}", [P, N // 2]) for h in range(2)]
        turn_p = pb("turn_p", [P, 2 * C])
        lin_p = pb("lin_p", [P, 2 * C])
        wh_p = pb("wh_p", [P, 2 * C])
        sum_p = pb("sum_p", [P, 2 * C])

        att_p = [score_p[q][:, 0:C] for q in range(2)]

        passed = sem("passed")
        weights_ld = sem("weights_ld")
        consts_done = sem("consts_done")
        weights_done = sem("weights_done")
        adj_ld = [sem(f"adj_ld{q}") for q in range(2)]
        cast_done = sem("cast_done")
        score_ready = sem("score_ready")
        score_used = sem("score_used")
        flag_put = sem("flag_put")
        flag_summed = sem("flag_summed")
        flag_ready = sem("flag_ready")
        again_dma = sem("again_dma")
        again_ld = sem("again_ld")
        again_used = sem("again_used")
        early_ready = sem("early_ready")
        late_ready = sem("late_ready")
        rows_ld = [sem(f"rows_ld{q}") for q in range(2)]
        rows_used0 = sem("rows_used0")
        rows_used = sem("rows_used")
        res_ready = sem("res_ready")
        res_out = [sem(f"res_out{q}") for q in range(2)]
        graph_out = sem("graph_out")
        redo_idx = sem("redo_idx")
        redo_dma = sem("redo_dma")
        redo_ld = sem("redo_ld")
        redo_res = sem("redo_res")
        redo_out = sem("redo_out")
        dense_go = sem("dense_go")
        dense_dma = sem("dense_dma")
        dense_tab = sem("dense_tab")
        dense_adj = sem("dense_adj")
        dense_mask = sem("dense_mask")
        dense_row = sem("dense_row")
        dense_e = sem("dense_e")
        dense_p = sem("dense_p")
        dense_turn = sem("dense_turn")
        dense_pt = sem("dense_pt")
        dense_att = sem("dense_att")
        dense_res = sem("dense_res")
        dense_out = sem("dense_out")
        pair_ld = [sem(f"pair_ld{q}") for q in range(2)]
        turned = sem("turned")
        h_ready = sem("h_ready")
        lin_ready = sem("lin_ready")
        var_ready = sem("var_ready")
        std_ready = sem("std_ready")
        x1_ready = sem("x1_ready")
        x1_turned = sem("x1_turned")
        x1t_ready = sem("x1t_ready")
        wh_ready = sem("wh_ready")
        tab_ready = sem("tab_ready")
        summed = sem("summed")
        mean_ready = sem("mean_ready")
        tab_out = [sem(f"tab_out{q}") for q in range(2)]
        table_ready = sem("table_ready")
        first_out = sem("first_out")
        logits_ready = sem("logits_ready")
        rows_weighted = sem("rows_weighted")
        exp_ready = sem("exp_ready")
        norm_ready = sem("norm_ready")
        elu_ready = sem("elu_ready")
        pair_used = sem("pair_used")
        final_ready = sem("final_ready")
        final_out = [sem(f"final_out{q}") for q in range(2)]

        def need(eng, s, value):
            if not isinstance(value, int) or value > 0:
                eng.wait_ge(s, value)

        def hold(eng, s, value):
            if not isinstance(value, int):
                eng.wait_ge(s, value)
                eng.sem_inc(passed, 1)
            elif value > 0:
                eng.wait_ge(s, value)

        half, hl = T // 2, T // 2 * LIST

        def landed(eng, dma_sem, count, to):
            eng.wait_ge(dma_sem, count)
            eng.sem_clear(dma_sem)
            eng.sem_inc(to, 1)

        def upto(u):
            return sum(SLOTS[u % 2:u + 1:2])

        def two_back(n, t):
            return n - 1 if t else n

        def tile_rows(b, t):
            return bass.ds(b * N + t * P, P)

        def program(eng, stage1, bridge, stage2):
            stage1(-1, True, False, False)
            stage1(0, True, True, False)
            with eng.Fori(1, B - 1) as b:
                stage1(b, True, True, True)
            stage1(B - 1, False, True, True)
            bridge()
            with eng.Fori(1, B - 1) as b:
                stage2(b, True, True)
            stage2(B - 1, True, True)
            stage2(B, False, True)

        block = ctx.enter_context(nc.Block())

        @block.sync
        def _(sp):
            sp.dma_start(w0_s[:, :, :], w0.rearrange("(c p) n -> p c n", p=P)).then_inc(weights_ld, 16)
            sp.dma_start(w1_s[:, :, 0:C], w1.rearrange("(c p) n -> p c n", p=P)).then_inc(weights_ld, 16)
            sp.dma_start(b0_s[:, :], b0.rearrange("(a n) -> a n", a=1)).then_inc(weights_ld, 16)
            sp.dma_start(a1_s[:, :], a1.rearrange("(a n) -> a n", a=1).broadcast_to([P, DH])).then_inc(weights_ld, 16)
            sp.dma_start(a2_s[:, :], a2.rearrange("(a n) -> a n", a=1).broadcast_to([P, DH])).then_inc(weights_ld, 16)
            sp.dma_start(gam[:, :], gamma.rearrange("(a n) -> a n", a=1).broadcast_to([P, C])).then_inc(weights_ld, 16)
            sp.dma_start(bet[:, :], beta.rearrange("(a n) -> a n", a=1).broadcast_to([P, C])).then_inc(weights_ld, 16)
            sp.wait_ge(consts_done, 1)
            sp.dma_start(b1_s[:, ROW:ROW + H], emb[1:2, :]).then_inc(weights_ld, 16)

            def load_adj(b, t):
                n, q = b * T + t, t % 2
                need(sp, cast_done, n - 1)
                sp.dma_start(adj_i[q][:, :], adj_rows[tile_rows(b, t), :]).then_inc(adj_ld[q], 16)

            def search_again(b):
                hold(sp, flag_ready, 2 * b + 1)
                over = sp.value_load(flag_i[0:1, bass.ds(2 * b, 1)])
                with sp.If(over > 0):
                    with sp.Fori(0, T) as t:
                        sp.wait_ge(again_used, b * T + t)
                        sp.dma_start(adj_i[0][:, :], adj_rows[bass.ds(b * N + t * P, P), :])\
                            .then_inc(again_dma, 16)
                        landed(sp, again_dma, 16, again_ld)
                with sp.Else():
                    sp.sem_inc(again_ld, T)
                hold(sp, again_used, T * (b + 1))

            def load_pair(b, t):
                n, q = b * T + t, t % 2
                if t == 0:
                    hold(sp, graph_out, b + 1)
                need(sp, x1_ready, two_back(n, t))
                sp.dma_start(pair[q][:, 0:C], x_rows[tile_rows(b, t), :]).then_inc(pair_ld[q], 16)
                sp.dma_start(pair[q][:, C:2 * C], agg_d[tile_rows(b, t), :]).then_inc(pair_ld[q], 16)

            def store_table(b, t):
                n, q = b * T + t, t % 2
                sp.wait_ge(tab_ready, n + 1)
                sp.dma_start(x1_d[tile_rows(b, t), :], x1[q][:, :]).then_inc(tab_out[q], 16)
                sp.dma_start(table_d[tile_rows(b, t), :], tab[q][:, :]).then_inc(tab_out[q], 16)
                if t == T - 1:
                    for q in range(2):
                        sp.wait_ge(tab_out[q], 16 * T * (b + 1))
                    sp.sem_inc(table_ready, 1)

            def stage1(b, search, reduce, finish):
                t_s = t_f = 0
                for u in range(T):
                    for _ in range(SEARCH[u] if search else 0):
                        load_adj(b + 1, t_s)
                        t_s += 1
                    if search and u == SORT_AT:
                        search_again(b + 1)
                    for _ in range(FINISH[u] if finish else 0):
                        if not t_f:
                            load_pair(b - 1, 0)
                        if t_f < T - 1:
                            load_pair(b - 1, t_f + 1)
                        if t_f:
                            store_table(b - 1, t_f - 1)
                        t_f += 1
                if finish:
                    store_table(b - 1, T - 1)

            def bridge():
                sp.wait_ge(table_ready, 1)
                sp.dma_start(first_d, table_d[0:N, :]).then_inc(first_out, 16)
                stage1(B, False, False, True)

            def dense(b):
                hold(sp, graph_out, B + b + 1)
                hold(sp, dense_go, b + 1)
                hold(sp, flag_ready, 2 * b + 2)
                many = sp.value_load(flag_i[0:1, bass.ds(2 * b + 1, 1)])
                with sp.If(many > 0):
                    sp.dma_start(graph_tab.rearrange("p (t c) -> p t c", c=ROW),
                                 table_d[bass.ds(b * N, N), :].rearrange("(t p) c -> p t c", p=P))\
                        .then_inc(dense_dma, 16)
                    landed(sp, dense_dma, 16, dense_tab)
                    with sp.Fori(0, T) as t:
                        sp.wait_ge(dense_mask, b * T + t)
                        sp.dma_start(adj_i[0][:, :], adj_rows[bass.ds(b * N + t * P, P), :])\
                            .then_inc(dense_dma, 16)
                        landed(sp, dense_dma, 16, dense_adj)
                        sp.wait_ge(dense_res, b * T + t + 1)
                        sp.dma_start(att_d[bass.ds(b * N + t * P, P), :], all_res[:, :])\
                            .then_inc(dense_dma, 16)
                        landed(sp, dense_dma, 16, dense_out)
                with sp.Else():
                    sp.sem_inc(dense_tab, 1)
                    sp.sem_inc(dense_adj, T)
                    sp.sem_inc(dense_out, T)

            def load_pair2(b, t):
                n, q = b * T + t, t % 2
                if t == 0:
                    hold(sp, graph_out, B + b + 1)
                need(sp, pair_used, two_back(n, t))
                sp.dma_start(pair[q][:, 0:C], att_d[tile_rows(b, t), :]).then_inc(pair_ld[q], 16)
                sp.dma_start(pair[q][:, C:2 * C], x1_d[tile_rows(b, t), :]).then_inc(pair_ld[q], 16)

            def store_final(b, t):
                n, q = b * T + t, t % 2
                sp.wait_ge(final_ready, n + 1)
                sp.dma_start(out_rows[tile_rows(b, t), :], x1[q][:, :]).then_inc(final_out[q], 16)

            def stage2(b, reduce, finish):
                t_f = 0
                for u in range(T):
                    for _ in range(FINISH[u] if finish else 0):
                        if not t_f:
                            dense(b - 1)
                            load_pair2(b - 1, 0)
                        if t_f < T - 1:
                            load_pair2(b - 1, t_f + 1)
                        if t_f:
                            store_final(b - 1, t_f - 1)
                        t_f += 1
                if finish:
                    store_final(b - 1, T - 1)

            program(sp, stage1, bridge, stage2)
            for q in range(2):
                sp.wait_ge(final_out[q], 16 * B * T // 2)

        @block.gpsimd
        def _(pool):
            steps = 0

            def step(last):
                nonlocal steps
                steps += 1
                last.then_inc(consts_done, 1)
                pool.wait_ge(consts_done, steps)

            step(pool.memset(b1_s[:, :], 0.0))
            step(pool.memset(ident[:, :], 0.0))
            step(pool.memset(ones[:, :], 1.0))
            step(pool.memset(mark_h[:, :], 0.0))
            step(pool.memset(ones_h[:, :], 1.0))
            step(pool.memset(cols_i[:, :], 0))
            for u in range(T):
                step(pool.memset(slots_c[:, u:u + 1], float(SLOTS[u])))
            step(pool.iota(c_i[:, 0:T], pattern=[[1, T]], base=0, channel_multiplier=0))
            step(pool.iota(c_i[:, T:T + LIST], pattern=[[1, LIST]], base=0, channel_multiplier=0))
            step(pool.iota(c_i[:, 48:49], pattern=[[0, 1]], base=0, channel_multiplier=1))
            step(pool.iota(c_i[:, 49:49 + B], pattern=[[N, B]], base=0, channel_multiplier=0))
            step(pool.iota(cols_i[0:1, :], pattern=[[-8, N // 8], [0, 8]], base=N, channel_multiplier=0))
            step(pool.iota(cols_i[32:33, :], pattern=[[0, N // 8], [-1, 8]], base=0, channel_multiplier=0))
            step(pool.affine_select(out=ident[:, :], in_=ident[:, :], compare_op=ALU.not_equal,
                                    fill=1.0, base=0, pattern=[[-1, P]], channel_multiplier=1))
            step(pool.affine_select(out=mark_h[:, :], in_=mark_h[:, :], compare_op=ALU.not_equal,
                                    fill=MARK, base=0, pattern=[[-1, P]], channel_multiplier=1))
            step(pool.tensor_copy(tno[:, :], c_i[:, 0:T]))
            step(pool.tensor_copy(kno[:, :], c_i[:, T:T + LIST]))
            step(pool.tensor_copy(row_p[:, :], c_i[:, 48:49]))
            step(pool.tensor_copy(base_b[:, :], c_i[:, 49:49 + B]))
            step(pool.tensor_copy(cols_h[:, :], cols_i[0:64, :]))
            step(pool.iota(cols_i[:, :], pattern=[[-1, N]], base=int(MARK) + N, channel_multiplier=0))
            step(pool.tensor_copy(value_row[:, :], cols_i[:, :]))
            step(pool.tensor_scalar(rev[:, :], tno[:, :], -1.0, float(T - 1), ALU.mult, ALU.add))
            assert steps == CONSTS

            redone = pool.alloc_register("redone")
            pool.reg_mov(redone, 0)

            def gather(b, u, table, width, order_b):
                n, q = order_b * T + u, u % 2
                if table is x_rows:
                    hold(pool, rows_used0, n - 1)
                elif isinstance(order_b, int) and order_b == B and u < 2:
                    pool.wait_ge(rows_used0, n - 1)
                else:
                    hold(pool, rows_used, n - B * T - 1)
                for k in range(SLOTS[u]):
                    at = u * LIST + k
                    pool.indirect_dma_start(
                        out=rows_g[q][:, k * width:(k + 1) * width], out_offset=None, in_=table,
                        in_offset=bass.IndirectOffsetOnAxis(ap=idx_cur[:, at:at + 1], axis=0),
                        bounds_check=B * N - 1, oob_is_err=False).then_inc(rows_ld[q], 16)

            def scatter(order_b, u, to):
                n, q = order_b * T + u, u % 2
                hold(pool, res_ready, n + 1)
                pool.indirect_dma_start(
                    out=to, out_offset=bass.IndirectOffsetOnAxis(ap=own_cur[:, u:u + 1], axis=0),
                    in_=res[q][:, :], in_offset=None, bounds_check=B * N - 1,
                    oob_is_err=False).then_inc(res_out[q], 16)

            def redo(b):
                hold(pool, flag_ready, 2 * b + 2)
                many = pool.value_load(flag_i[0:1, bass.ds(2 * b + 1, 1)])
                with pool.If(many > 0):
                    for q in range(2):
                        hold(pool, res_out[q], 16 * half * (b + 1))
                    with pool.Fori(0, T) as u:
                        hold(pool, redo_idx, b * T + u + 1)
                        for k in range(TOP):
                            pool.indirect_dma_start(
                                out=all_g[:, k * C:(k + 1) * C], out_offset=None, in_=x_rows,
                                in_offset=bass.IndirectOffsetOnAxis(ap=all_idx[:, k:k + 1], axis=0),
                                bounds_check=B * N - 1, oob_is_err=False).then_inc(redo_dma, 16)
                        pool.reg_add(redone, redone, 16 * TOP)
                        pool.wait_ge(redo_dma, redone)
                        pool.sem_inc(redo_ld, 1)
                        hold(pool, redo_res, b * T + u + 1)
                        pool.indirect_dma_start(
                            out=agg_d, out_offset=bass.IndirectOffsetOnAxis(ap=all_own[:, :], axis=0),
                            in_=all_res[:, :], in_offset=None, bounds_check=B * N - 1,
                            oob_is_err=False).then_inc(redo_dma, 16)
                        pool.reg_add(redone, redone, 16)
                        pool.wait_ge(redo_dma, redone)
                        pool.sem_inc(redo_out, 1)
                with pool.Else():
                    pool.sem_inc(redo_ld, T)
                    pool.sem_inc(redo_out, T)

            def end_graph(order_b):
                for q in range(2):
                    hold(pool, res_out[q], 16 * (T // 2) * (order_b + 1))
                pool.sem_inc(graph_out, 1)

            def stage1(b, search, reduce, finish):
                for u in range(T if reduce else 0):
                    if u == 0:
                        hold(pool, early_ready, b + 1)
                    if u == T // 2:
                        hold(pool, late_ready, b + 1)
                    gather(b, u, x_rows, C, b)
                    if u == 0 and finish:
                        scatter(b - 1, T - 1, agg_d)
                        redo(b - 1)
                        end_graph(b - 1)
                    if u:
                        scatter(b, u - 1, agg_d)

            def bridge():
                pool.wait_ge(early_ready, B + 1)
                pool.wait_ge(first_out, 16)
                gather(0, 0, first_d, ROW, B)
                scatter(B - 1, T - 1, agg_d)
                redo(B - 1)
                end_graph(B - 1)
                for u in range(1, T):
                    if u == T // 2:
                        pool.wait_ge(late_ready, B + 1)
                    gather(0, u, first_d, ROW, B)
                    scatter(B, u - 1, att_d)

            def stage2(b, reduce, finish):
                for u in range(T if reduce else 0):
                    if u == 0:
                        hold(pool, early_ready, B + b + 1)
                        pool.wait_ge(table_ready, B)
                    if u == T // 2:
                        hold(pool, late_ready, B + b + 1)
                    gather(b, u, table_d, ROW, B + b)
                    if u == 0 and finish:
                        scatter(B + b - 1, T - 1, att_d)
                        end_graph(B + b - 1)
                    if u:
                        scatter(B + b, u - 1, att_d)
                if finish and not reduce:
                    scatter(B + b - 1, T - 1, att_d)
                    end_graph(B + b - 1)

            program(pool, stage1, bridge, stage2)

        @block.scalar
        def _(act):
            def cast(b, t):
                n, q = b * T + t, t % 2
                act.wait_ge(adj_ld[q], 16 * (b * (T // 2) + t // 2 + 1))
                need(act, score_ready, 2 * n - 2)
                act.activation(adj_h[q], adj_i[q][:, :], ACT.Copy,
                               accum_out=degree[:, bass.ds(n, 1)]).then_inc(cast_done, 1)

            def finish_a(b, t):
                n = b * T + t
                act.wait_ge(turned, n + 1)
                need(act, lin_ready, n)
                act.activation(h_t[:, :], turn_p[:, :], ACT.Copy).then_inc(h_ready, 1)

            def finish_b(b, t):
                n, q = b * T + t, t % 2
                act.wait_ge(x1_turned, n + 1)
                need(act, wh_ready, n)
                act.activation(x1_t[:, :], turn_p[:, 0:C], ACT.Copy).then_inc(x1t_ready, 1)
                act.wait_ge(wh_ready, n + 1)
                need(act, tab_out[q], 16 * (b * T + t // 2 * 2))
                need(act, summed, two_back(n, t))
                act.activation(tab[q][:, :], wh_p[:, 0:ROW], ACT.Copy)
                act.activation(self_s[:, bass.ds(n * H, H)], wh_p[:, ROW:ROW + H], ACT.Copy)\
                    .then_inc(tab_ready, 1)
                if t == T - 1:
                    act.wait_ge(summed, n + 1)
                    act.activation(mean_wh[:, bass.ds(b * C, C)], sum_p[:, 0:C], ACT.Copy,
                                   scale=1.0 / N).then_inc(mean_ready, 1)

            def finish(b, t):
                finish_a(b, t)
                if t:
                    finish_b(b, t - 1)
                act.wait_ge(var_ready, b * T + t + 1)
                act.activation(std[:, 0:1], var[:, 0:1], ACT.Sqrt).then_inc(std_ready, 1)
                if t == T - 1:
                    finish_b(b, t)

            def stage1(b, search, reduce, finish_):
                t_s = t_f = 0
                for u in range(T):
                    for _ in range(SEARCH[u] if search else 0):
                        cast(b + 1, t_s)
                        t_s += 1
                    for _ in range(FINISH[u] if finish_ else 0):
                        finish(b - 1, t_f)
                        t_f += 1

            def bridge():
                t_f = 0
                for u in range(T):
                    for _ in range(FINISH[u]):
                        finish(B - 1, t_f)
                        t_f += 1
                    exps(0, u)

            def exps(b, u):
                n, w = b * T + u, SLOTS[u] * H
                act.wait_ge(logits_ready, n + 1)
                act.activation(pr[:, 0:w], e[:, 0:w], ACT.Exp).then_inc(exp_ready, 1)

            def elu(b, t):
                n = b * T + t
                act.wait_ge(norm_ready, n + 1)
                act.activation(neg[:, :], z[:, :], ACT.Relu, scale=-1.0)
                act.drain()
                act.activation(neg[:, :], neg[:, :], ACT.Exp, scale=-1.0).then_inc(elu_ready, 1)

            def root(b, j):
                act.wait_ge(var_ready, B * T + b * (T + 1) + j + 1)
                act.activation(std[:, :], var[:, :], ACT.Sqrt).then_inc(std_ready, 1)

            def dense(b):
                hold(act, dense_out, T * b)
                act.wait_ge(flag_ready, 2 * b + 2)
                many = act.value_load(flag_i[0:1, bass.ds(2 * b + 1, 1)])
                with act.If(many > 0):
                    with act.Fori(0, T) as t:
                        with act.Fori(0, H) as h:
                            m = (b * T + t) * H + h
                            act.wait_ge(dense_res, b * T + t)
                            act.wait_ge(dense_e, m + 1)
                            act.activation(heat, heat, ACT.Exp, bias=peak[:, 0:1],
                                           accum_out=sums[:, bass.ds(h, 1)]).then_inc(dense_p, 1)
                            act.wait_ge(dense_att, m)
                            for g in range(4):
                                act.wait_ge(dense_turn, 4 * m + g + 1)
                                act.activation(heat_t[:, 512 * g:512 * (g + 1)], turn_p[:, :],
                                               ACT.Copy).then_inc(dense_pt, 1)
                with act.Else():
                    act.sem_inc(dense_p, T * H)
                    act.sem_inc(dense_pt, 4 * T * H)

            def stage2(b, reduce, finish):
                t_f = 0
                dense(b - 1)
                for u in range(T):
                    if FINISH[u] and not t_f:
                        root(b - 1, 0)
                    if reduce:
                        exps(b, u)
                    for _ in range(FINISH[u]):
                        elu(b - 1, t_f)
                        t_f += 1
                        root(b - 1, t_f)

            program(act, stage1, bridge, stage2)

        @block.tensor
        def _(pe):
            pe.wait_ge(consts_done, CONSTS)
            pe.wait_ge(weights_ld, 16 * 8)
            pe.wait_ge(weights_done, 1)

            def scores(b, t):
                n, q = b * T + t, t % 2
                pe.wait_ge(cast_done, n + 1)
                for h in range(2):
                    need(pe, score_used, 2 * n + h - 1)
                    for c in range(2):
                        o = score_p[h][:, 512 * c:512 * (c + 1)]
                        at = slice(1024 * h + 512 * c, 1024 * h + 512 * (c + 1))
                        pe.matmul(o, mark_h[:, :], adj_h[q][:, at], start=True, stop=False)
                        last = pe.matmul(o, ones_h[:, :], cols_h[:, at], start=False, stop=True)
                    last.then_inc(score_ready, 1)

            def sum_flag(k, col):
                pe.wait_ge(flag_put, k)
                pe.matmul(wh_p[0:1, 2 * C - 2 + col:2 * C - 1 + col], ones[:, 0:1],
                          flag_in[:, col:col + 1], start=True, stop=True).then_inc(flag_summed, 1)
                pe.wait_ge(flag_ready, k)

            def finish_a(b, t):
                n, q = b * T + t, t % 2
                pe.wait_ge(pair_ld[q], 16 * (b * T + t // 2 * 2 + 2))
                need(pe, x1t_ready, n - 1 if t > 1 else b * T)
                for c in range(4):
                    last = pe.transpose(turn_p[:, P * c:P * (c + 1)], pair[q][:, P * c:P * (c + 1)],
                                        ident[:, :])
                last.then_inc(turned, 1)
                pe.wait_ge(h_ready, n + 1)
                need(pe, x1_ready, n)
                pe.matmul(lin_p[:, 0:C], ones[0:1, :], b0_s[0:1, :], start=True, stop=False)
                for c in range(4):
                    last = pe.matmul(lin_p[:, 0:C], h_t[:, P * c:P * (c + 1)], w0_s[:, c, :],
                                     start=False, stop=(c == 3))
                last.then_inc(lin_ready, 1)

            def finish_b(b, t):
                n, q = b * T + t, t % 2
                pe.wait_ge(x1_ready, n + 1)
                for c in range(2):
                    last = pe.transpose(turn_p[:, P * c:P * (c + 1)], x1[q][:, P * c:P * (c + 1)],
                                        ident[:, :])
                last.then_inc(x1_turned, 1)
                pe.wait_ge(x1t_ready, n + 1)
                need(pe, tab_ready, n)
                pe.matmul(wh_p[:, 0:ROW + H], ones[0:1, :], b1_s[0:1, :], start=True, stop=False)
                for c in range(2):
                    last = pe.matmul(wh_p[:, 0:ROW + H], x1_t[:, P * c:P * (c + 1)], w1_s[:, c, :],
                                     start=False, stop=(c == 1))
                last.then_inc(wh_ready, 1)
                pe.wait_ge(tab_ready, n + 1)
                if t == 0:
                    need(pe, mean_ready, b)
                pe.matmul(sum_p[:, 0:C], ones[:, :], tab[q][:, 0:C], start=(t == 0),
                          stop=(t == T - 1)).then_inc(summed, 1)

            def finish(b, t):
                finish_a(b, t)
                if t:
                    finish_b(b, t - 1)
                if t == T - 1:
                    finish_b(b, t)

            def attend(b, u):
                n, q = (B + b) * T + u, u % 2
                pe.wait_ge(rows_weighted, b * T + u + 1)
                need(pe, res_ready, n - 1)
                for k in range(SLOTS[u]):
                    last = pe.matmul(att_p[q], ident[:, :], rows_g[q][:, k * ROW:k * ROW + C],
                                     start=(k == 0), stop=(k == SLOTS[u] - 1))
                last.then_inc(rows_used, 1)

            def stage1(b, search, reduce, finish_):
                t_s = t_f = 0
                for u in range(T):
                    for _ in range(SEARCH[u] if search else 0):
                        scores(b + 1, t_s)
                        t_s += 1
                    if search and u == SORT_AT:
                        sum_flag(2 * b + 3, 0)
                        sum_flag(2 * b + 4, 1)
                    for _ in range(FINISH[u] if finish_ else 0):
                        finish(b - 1, t_f)
                        t_f += 1

            def bridge():
                t_f = 0
                for u in range(T):
                    for _ in range(FINISH[u]):
                        finish(B - 1, t_f)
                        t_f += 1
                    attend(0, u)

            def dense(b):
                hold(pe, dense_out, T * b)
                pe.wait_ge(flag_ready, 2 * b + 2)
                many = pe.value_load(flag_i[0:1, bass.ds(2 * b + 1, 1)])
                with pe.If(many > 0):
                    hold(pe, dense_tab, b + 1)
                    with pe.Fori(0, T) as t:
                        for h in range(H):
                            m = (b * T + t) * H + h
                            pe.wait_ge(dense_e, m)
                            for c in range(T):
                                last = pe.matmul(
                                    score_p[c // 8][:, P * (c % 8):P * (c % 8 + 1)],
                                    graph_tab[:, c * ROW + C + h:c * ROW + C + h + 1].broadcast_to([P, P]),
                                    ident[:, :], start=True, stop=True)
                            last.then_inc(dense_row, 1)
                            pe.wait_ge(dense_p, m + 1)
                            for g in range(4):
                                pe.wait_ge(dense_pt, 4 * m + g)
                                for c in range(4 * g, 4 * g + 4):
                                    last = pe.transpose(turn_p[:, P * (c % 4):P * (c % 4 + 1)],
                                                        heat[:, P * c:P * (c + 1)], ident[:, :])
                                last.then_inc(dense_turn, 1)
                            pe.wait_ge(dense_pt, 4 * m + 4)
                            pe.wait_ge(dense_res, b * T + t)
                            for c in range(T):
                                last = pe.matmul(sum_p[:, h * DH:(h + 1) * DH],
                                                 heat_t[:, P * c:P * (c + 1)],
                                                 graph_tab[:, c * ROW + h * DH:c * ROW + (h + 1) * DH],
                                                 start=(c == 0), stop=(c == T - 1))
                            last.then_inc(dense_att, 1)
                with pe.Else():
                    pe.sem_inc(dense_row, T * H)
                    pe.sem_inc(dense_turn, 4 * T * H)
                    pe.sem_inc(dense_att, T * H)

            def stage2(b, reduce, finish_):
                dense(b - 1)
                for u in range(T if reduce else 0):
                    attend(b, u)

            program(pe, stage1, bridge, stage2)

        @block.vector
        def _(dve):
            v = nc.vector

            def settle():
                v.drain()

            v.memset(var[:, :], 1.0)
            dve.wait_ge(weights_ld, 16 * 8)
            for a_s, to in ((a2_s, C), (a1_s, ROW)):
                for c in range(2):
                    prod = wide[:, C * c:C * (c + 1)].rearrange("p (h d) -> p h d", d=DH)
                    v.tensor_tensor(prod, w1_s[:, c, 0:C].rearrange("p (h d) -> p h d", d=DH),
                                    a_s[:, :].unsqueeze(1).broadcast_to([P, H, DH]), ALU.mult)
                settle()
                for c in range(2):
                    prod = wide[:, C * c:C * (c + 1)].rearrange("p (h d) -> p h d", d=DH)
                    v.tensor_reduce(w1_s[:, c, to:to + H], prod, AX, ALU.add)
                settle()
            v.drain().then_inc(weights_done, 1)
            dve.wait_ge(consts_done, CONSTS)

            def top_lists(src, put):
                for r in range(4):
                    v.max(put(r), src)
                    settle()
                    if r < 3:
                        v.match_replace(src, put(r), src, 0.0)
                        settle()

            def search(b, t):
                n = b * T + t
                settle()
                for h in range(2):
                    hold(dve, score_ready, 2 * n + h + 1)
                    for c in range(8):
                        at = 8 * (8 * h + c)
                        last = v.max(cand[:, at:at + 8], score_p[h][:, CH * c:CH * (c + 1)])
                    last.then_inc(score_used, 1)
                settle()
                v.tensor_reduce(eighth[:, t:t + 1],
                                cand[:, :].rearrange("p (c k) -> p c k", k=8)[:, :, 7], AX, ALU.max)
                settle()
                top_lists(cand[:, :], lambda r: lists[:, t * LIST + 8 * r:t * LIST + 8 * r + 8])

            def search_again(b):
                settle()
                v.tensor_reduce(flag_in[:, 1:2], eighth[:, :], AX, ALU.max)
                settle()
                v.tensor_scalar(flag_in[:, 0:1], flag_in[:, 1:2], MARK, None, ALU.is_gt)\
                    .then_inc(flag_put, 1)
                hold(dve, flag_summed, 2 * b + 1)
                v.tensor_copy(flag_i[0:1, bass.ds(2 * b, 1)], wh_p[0:1, 2 * C - 2:2 * C - 1])\
                    .then_inc(flag_ready, 1)
                hold(dve, flag_ready, 2 * b + 1)
                over = dve.value_load(flag_i[0:1, bass.ds(2 * b, 1)])
                with dve.If(over > 0):
                    with dve.Fori(0, T) as t:
                        dve.wait_ge(again_ld, b * T + t + 1)
                        v.tensor_tensor(wide[:, 0:N], adj_i[0][:, :], value_row[:, :], ALU.mult)\
                            .then_inc(again_used, 1)
                        settle()
                        top_lists(wide[:, 0:N], lambda r: top[:, 8 * r:8 * r + 8])
                        settle()
                        v.tensor_copy(lists[:, bass.ds(t * LIST, LIST)], top[:, :])
                        settle()
                with dve.Else():
                    dve.sem_inc(again_used, T)

            def sort(b):
                at, cur = bass.ds(b * T, T), bass.ds(b * T * LIST, T * LIST)
                v.scalar_tensor_tensor(key[:, :], degree[:, at], float(T), rev[:, :],
                                       ALU.mult, ALU.add)
                settle()
                v.max(order[:, 0:8], key[:, :])
                settle()
                v.match_replace(key2[:, :], order[:, 0:8], key[:, :], -1.0)
                settle()
                v.max(order[:, 8:16], key2[:, :])
                settle()
                pick = picks[:, bass.ds(b * T * T, T * T)].rearrange("p (u t) -> p u t", t=T)
                v.tensor_tensor(pick, order[:, :].unsqueeze(2).broadcast_to([P, T, T]),
                                key[:, :].unsqueeze(1).broadcast_to([P, T, T]), ALU.is_equal)
                settle()
                prod = wide[:, :].rearrange("p (u k t) -> p u k t", k=LIST, t=T)
                v.tensor_tensor(prod, pick.unsqueeze(2).broadcast_to([P, T, LIST, T]),
                                lists[:, :].rearrange("p (t k) -> p k t", k=LIST).unsqueeze(1)
                                .broadcast_to([P, T, LIST, T]), ALU.mult)
                prod2 = small[:, :].rearrange("p (u t) -> p u t", t=T)
                v.tensor_tensor(prod2, pick, tno[:, :].unsqueeze(1).broadcast_to([P, T, T]), ALU.mult)
                settle()
                v.tensor_reduce(moved[:, :], wide[:, :].rearrange("p (a t) -> p a t", t=T), AX, ALU.add)
                v.tensor_reduce(tile_of[:, :], prod2, AX, ALU.add)
                settle()
                first = moved[:, :].rearrange("p (u k) -> p u k", k=LIST)[:, :, 0:1]\
                    .broadcast_to([P, T, LIST])
                m3 = moved[:, :].rearrange("p (u k) -> p u k", k=LIST)
                v.scalar_tensor_tensor(fill[:, :].rearrange("p (u k) -> p u k", k=LIST), m3, MARK,
                                       first, ALU.is_le, ALU.mult)
                v.tensor_tensor(order[:, :], order[:, :], tile_of[:, :], ALU.add)
                v.tensor_scalar(own[:, :], tile_of[:, :], float(P), row_p[:, 0:1], ALU.mult, ALU.add)
                settle()
                v.scalar_tensor_tensor(moved[:, :], moved[:, :], MARK, moved[:, :],
                                       ALU.is_gt, ALU.mult)
                v.tensor_scalar(deg_all[:, at], order[:, :], float(T - 1), 1.0 / T,
                                ALU.subtract, ALU.mult)
                v.tensor_scalar(own_all[:, at], own[:, :], base_b[:, bass.ds(b, 1)], None, ALU.add)
                settle()
                v.tensor_tensor(moved[:, :], moved[:, :], fill[:, :], ALU.add)
                v.tensor_scalar(low_all[:, at], deg_all[:, at], float(TOP), LOWEST, ALU.is_gt, ALU.mult)
                v.tensor_scalar(has_all[:, at], deg_all[:, at], 0.5, None, ALU.is_gt)
                v.tensor_scalar(hasnt_all[:, at], deg_all[:, at], 0.5, None, ALU.is_lt)
                v.tensor_tensor(key[:, :], deg_all[:, at], slots_c[:, :], ALU.subtract)
                settle()
                v.tensor_scalar(moved[:, :], moved[:, :], -1.0, MARK + N, ALU.mult, ALU.add)
                v.tensor_reduce(key2[:, 0:1], key[:, :], AX, ALU.max)
                settle()
                v.tensor_scalar(idx_all[:, cur], moved[:, :], float(N - 1), base_b[:, bass.ds(b, 1)],
                                ALU.min, ALU.add)
                v.tensor_scalar(flag_in[:, 1:2], key2[:, 0:1], 0.0, None, ALU.is_gt)\
                    .then_inc(flag_put, 1)
                hold(dve, flag_summed, 2 * b + 2)
                v.tensor_copy(flag_i[0:1, bass.ds(2 * b + 1, 1)], wh_p[0:1, 2 * C - 1:2 * C])\
                    .then_inc(flag_ready, 1)

            def early_lists(b, order_b):
                settle()
                hold(dve, rows_ld[1], 16 * ((order_b - 1) * upto(T - 1) + upto(half - 1)))
                hold(dve, res_out[0], 16 * ((order_b - 1) * half + half // 2))
                hold(dve, res_out[1], 16 * ((order_b - 1) * half + half // 2))
                v.tensor_copy(idx_cur[:, 0:hl], idx_all[:, bass.ds(b * T * LIST, hl)])
                v.tensor_copy(own_cur[:, 0:half], own_all[:, bass.ds(b * T, half)]).then_inc(early_ready, 1)

            def late_lists(b, order_b):
                hold(dve, res_out[0], 16 * (order_b * half))
                hold(dve, res_out[1], 16 * (order_b * half))
                v.tensor_copy(idx_cur[:, hl:2 * hl], idx_all[:, bass.ds(b * T * LIST + hl, hl)])
                v.tensor_copy(own_cur[:, half:T], own_all[:, bass.ds(b * T + half, half)])\
                    .then_inc(late_ready, 1)

            def wait_rows(order_b, u):
                q = u % 2
                dve.wait_ge(rows_ld[q], 16 * (order_b * upto(T - 2 + q) + upto(u)))

            def max_tile(b, u):
                n, q, k = b * T + u, u % 2, SLOTS[u]
                settle()
                wait_rows(b, u)
                v.tensor_reduce(y[:, :], rows_g[q][:, 0:k * C].rearrange("p (k c) -> p c k", c=C),
                                AX, ALU.max).then_inc(rows_used0, 1)
                hold(dve, res_out[q], 16 * (b * half + u // 2))
                settle()
                v.tensor_scalar(res[q][:, :], y[:, :], low_all[:, bass.ds(n, 1)],
                                has_all[:, bass.ds(n, 1)], ALU.max, ALU.mult).then_inc(res_ready, 1)

            def variance(src, j, last=None):
                v.bn_stats(stats[:, 6 * j:6 * j + 6], src)
                settle()
                v.bn_aggr(mv[:, 2 * j:2 * j + 2], stats[:, 6 * j:6 * j + 6])
                settle()
                return v.tensor_scalar(var[:, j:j + 1], mv[:, 2 * j + 1:2 * j + 2], EPS, None, ALU.add)

            def normal(dst, src, j):
                return v.tensor_scalar(dst, src, mv[:, 2 * j:2 * j + 1], rstd[:, j:j + 1],
                                       ALU.subtract, ALU.mult)

            def finish_a(b, t):
                n, q = b * T + t, t % 2
                settle()
                hold(dve, lin_ready, n + 1)
                v.scalar_tensor_tensor(z[:, :], lin_p[:, 0:C], 0.0, pair[q][:, 0:C], ALU.max, ALU.add)
                settle()
                variance(z[:, :], 0).then_inc(var_ready, 1)

            def finish_b(b, t):
                n, q = b * T + t, t % 2
                dve.wait_ge(std_ready, n + 1)
                v.reciprocal(rstd[:, 0:1], std[:, 0:1])
                hold(dve, tab_out[q], 16 * (b * T + t // 2 * 2))
                settle()
                hold(dve, x1_turned, two_back(n, t))
                normal(x1[q][:, :], z[:, :], 0).then_inc(x1_ready, 1)

            def redo(b):
                settle()
                hold(dve, redo_out, T * b)
                hold(dve, flag_ready, 2 * b + 2)
                many = dve.value_load(flag_i[0:1, bass.ds(2 * b + 1, 1)])
                with dve.If(many > 0):
                    with dve.Fori(0, T) as u:
                        n = b * T + u
                        hold(dve, redo_out, n)
                        v.tensor_copy(all_idx[:, :], idx_all[:, bass.ds(n * LIST, LIST)])
                        v.tensor_copy(all_own[:, :], own_all[:, bass.ds(n, 1)])
                        v.drain().then_inc(redo_idx, 1)
                        hold(dve, redo_ld, n + 1)
                        v.tensor_reduce(y[:, :], all_g.rearrange("p (k c) -> p c k", c=C),
                                        AX, ALU.max)
                        settle()
                        v.tensor_scalar(all_res[:, :], y[:, :], low_all[:, bass.ds(n, 1)],
                                        has_all[:, bass.ds(n, 1)], ALU.max, ALU.mult)
                        v.drain().then_inc(redo_res, 1)
                with dve.Else():
                    dve.sem_inc(redo_idx, T)
                    dve.sem_inc(redo_res, T)
                settle()

            def stage1(b, search_, reduce, finish):
                t_s = t_f = 0
                for u in range(T):
                    for _ in range(SEARCH[u] if search_ else 0):
                        search(b + 1, t_s)
                        t_s += 1
                    if search_ and u == SORT_AT:
                        search_again(b + 1)
                        sort(b + 1)
                        settle()
                        early_lists(b + 1, b + 1)
                    if reduce and u == LATE_AT:
                        late_lists(b, b)
                    f = FINISH[u] if finish else 0
                    if f:
                        finish_a(b - 1, t_f)
                    if reduce:
                        max_tile(b, u)
                    if finish and u == 0:
                        redo(b - 1)
                    for i in range(f):
                        if i:
                            finish_a(b - 1, t_f)
                        finish_b(b - 1, t_f)
                        t_f += 1
                    if u == SORT_AT and reduce and not search_:
                        early_lists(0, B)

            def graph_terms(b):
                settle()
                prod = wide[:, 0:T * H * T].rearrange("p (u h t) -> p u h t", h=H, t=T)
                pick = picks[:, bass.ds(b * T * T, T * T)].rearrange("p (u t) -> p u t", t=T)
                v.tensor_tensor(prod, pick.unsqueeze(2).broadcast_to([P, T, H, T]),
                                self_s[:, bass.ds(b * T * H, T * H)]
                                .rearrange("p (t h) -> p h t", h=H).unsqueeze(1)
                                .broadcast_to([P, T, H, T]), ALU.mult)
                v.tensor_tensor(far_cur[:, :].rearrange("p (u k) -> p u k", k=LIST),
                                kno[:, :].unsqueeze(1).broadcast_to([P, T, LIST]),
                                deg_all[:, bass.ds(b * T, T)].unsqueeze(2).broadcast_to([P, T, LIST]),
                                ALU.is_ge)
                settle()
                v.tensor_reduce(self_cur[:, :], wide[:, 0:T * H * T].rearrange("p (a t) -> p a t", t=T),
                                AX, ALU.add)
                v.tensor_scalar(far_cur[:, :], far_cur[:, :], FAR, None, ALU.mult)
                settle()

            def weights(b, u, fb, ft):
                q, k = u % 2, SLOTS[u]
                g3 = rows_g[q][:, 0:k * ROW].rearrange("p (k c) -> p k c", c=ROW)
                e3 = e[:, 0:k * H].rearrange("p (k h) -> p k h", h=H)
                item = ft is not None
                settle()
                if item:
                    hold(dve, std_ready, B * T + fb * (T + 1) + ft + 1)
                    v.reciprocal(rstd[:, :], std[:, :])
                if b is not None:
                    wait_rows(B + b, u)
                    v.tensor_tensor(e3, g3[:, :, C:ROW], self_cur[:, u * H:(u + 1) * H].unsqueeze(1)
                                    .broadcast_to([P, k, H]), ALU.add)
                if item and ft:
                    hold(dve, final_out[1 - ft % 2], 16 * (fb * half + (ft - 1) // 2))
                settle()
                if b is not None:
                    v.scalar_tensor_tensor(e[:, 0:k * H], e[:, 0:k * H], 0.2, e[:, 0:k * H],
                                           ALU.mult, ALU.max)
                if item:
                    normal(z[:, :], pair[ft % 2][:, 0:C], 0)
                    if ft:
                        normal(x1[1 - ft % 2][:, :], y2[:, :], 1).then_inc(final_ready, 1)
                settle()
                if b is not None:
                    v.tensor_tensor(e3, e3, far_cur[:, u * LIST:u * LIST + k].unsqueeze(2)
                                    .broadcast_to([P, k, H]), ALU.add)
                if item:
                    v.tensor_tensor(z[:, :], z[:, :], gam[:, :], ALU.mult)
                settle()
                if b is not None:
                    v.tensor_reduce(mx[:, :], e3.rearrange("p k h -> p h k"), AX, ALU.max)
                if item:
                    v.tensor_tensor(z[:, :], z[:, :], bet[:, :], ALU.add).then_inc(norm_ready, 1)
                if b is not None:
                    settle()
                    v.tensor_tensor(e3, e3, mx[:, :].unsqueeze(1).broadcast_to([P, k, H]),
                                    ALU.subtract).then_inc(logits_ready, 1)

            def combine(b, u):
                n, q = b * T + u, u % 2
                hold(dve, res_out[q], 16 * ((B + b) * half + u // 2))
                hold(dve, rows_used, n + 1)
                v.scalar_tensor_tensor(res[q][:, :], mean_wh[:, bass.ds(b * C, C)],
                                       hasnt_all[:, bass.ds(n, 1)], att_p[q], ALU.mult, ALU.add)\
                    .then_inc(res_ready, 1)

            def attend(b, u, fb, ft):
                item = ft is not None
                if b is not None:
                    n, q, k = b * T + u, u % 2, SLOTS[u]
                    g3 = rows_g[q][:, 0:k * ROW].rearrange("p (k c) -> p k c", c=ROW)
                    p3 = pr[:, 0:k * H].rearrange("p (k h) -> p k h", h=H)
                    if u:
                        combine(b, u - 1)
                    hold(dve, exp_ready, n + 1)
                    v.tensor_reduce(su[:, :], p3.rearrange("p k h -> p h k"), AX, ALU.add)
                settle()
                if b is not None:
                    v.reciprocal(su[:, :], su[:, :])
                if item:
                    hold(dve, elu_ready, fb * T + ft + 1)
                    v.scalar_tensor_tensor(y2[:, :], z[:, :], 0.0, neg[:, :], ALU.max, ALU.add)
                settle()
                if b is not None:
                    v.tensor_scalar(su[:, :], su[:, :], has_all[:, bass.ds(n, 1)], None, ALU.mult)
                if item:
                    v.scalar_tensor_tensor(y2[:, :], y2[:, :], -1.0, pair[ft % 2][:, C:2 * C],
                                           ALU.add, ALU.add).then_inc(pair_used, 1)
                settle()
                if b is not None:
                    v.tensor_tensor(p3, p3, su[:, :].unsqueeze(1).broadcast_to([P, k, H]), ALU.mult)
                if item:
                    if ft < T - 1:
                        wait_pair(fb, ft + 1)
                        v.bn_stats(stats[:, 0:6], pair[1 - ft % 2][:, 0:C])
                    v.bn_stats(stats[:, 6:12], y2[:, :])
                settle()
                if b is not None:
                    g4 = g3[:, :, 0:C].rearrange("p k (h d) -> p k h d", d=DH)
                    v.tensor_tensor(g4, g4, p3.unsqueeze(3).broadcast_to([P, k, H, DH]), ALU.mult)\
                        .then_inc(rows_weighted, 1)
                if item:
                    for j in range(0 if ft < T - 1 else 1, 2):
                        v.bn_aggr(mv[:, 2 * j:2 * j + 2], stats[:, 6 * j:6 * j + 6])
                    settle()
                    for j in range(0 if ft < T - 1 else 1, 2):
                        v.tensor_scalar(var[:, j:j + 1], mv[:, 2 * j + 1:2 * j + 2], EPS, None, ALU.add)
                    v.drain().then_inc(var_ready, 1)

            def wait_pair(b, t):
                hold(dve, pair_ld[t % 2], 16 * (B * T + b * T + t // 2 * 2 + 2))

            def last_norm(b):
                hold(dve, std_ready, B * T + (b + 1) * (T + 1))
                settle()
                v.reciprocal(rstd[:, :], std[:, :])
                hold(dve, final_out[1], 16 * (b * half + half - 1))
                settle()
                normal(x1[1][:, :], y2[:, :], 1).then_inc(final_ready, 1)

            def dense(b):
                hold(dve, dense_out, T * b)
                v.drain().then_inc(dense_go, 1)
                hold(dve, flag_ready, 2 * b + 2)
                many = dve.value_load(flag_i[0:1, bass.ds(2 * b + 1, 1)])
                with dve.If(many > 0):
                    with dve.Fori(0, T) as t:
                        n = b * T + t
                        hold(dve, dense_adj, n + 1)
                        hold(dve, dense_turn, 4 * H * n)
                        v.tensor_scalar(mask, adj_i[0][:, :], -FAR, FAR, ALU.mult, ALU.add)\
                            .then_inc(dense_mask, 1)
                        settle()
                        with dve.Fori(0, H) as h:
                            m = n * H + h
                            hold(dve, dense_turn, 4 * m)
                            hold(dve, dense_row, m + 1)
                            for g in range(2):
                                v.tensor_scalar(heat[:, 1024 * g:1024 * (g + 1)], score_p[g][:, :],
                                                self_s[:, bass.ds(m, 1)], None, ALU.add)
                            settle()
                            v.scalar_tensor_tensor(heat, heat, 0.2, heat, ALU.mult, ALU.max)
                            settle()
                            v.tensor_tensor(heat, heat, mask, ALU.add)
                            settle()
                            v.tensor_reduce(peak[:, :], heat, AX, ALU.max)
                            settle()
                            v.tensor_scalar(peak[:, :], peak[:, :], -1.0, None, ALU.mult)
                            v.drain().then_inc(dense_e, 1)
                        v.tensor_scalar(lone[:, 0:1], degree[:, bass.ds(n, 1)], 0.5, None, ALU.is_gt)
                        v.tensor_scalar(lone[:, 1:2], degree[:, bass.ds(n, 1)], 0.5, None, ALU.is_lt)
                        hold(dve, dense_att, H * (n + 1))
                        hold(dve, dense_out, n)
                        v.reciprocal(su[:, :], sums[:, :])
                        settle()
                        v.tensor_scalar(su[:, :], su[:, :], lone[:, 0:1], None, ALU.mult)
                        settle()
                        v.tensor_tensor(y[:, :].rearrange("p (h d) -> p h d", d=DH),
                                        sum_p[:, 0:C].rearrange("p (h d) -> p h d", d=DH),
                                        su[:, :].unsqueeze(2).broadcast_to([P, H, DH]), ALU.mult)
                        settle()
                        v.scalar_tensor_tensor(all_res[:, :], mean_wh[:, bass.ds(b * C, C)],
                                               lone[:, 1:2], y[:, :], ALU.mult, ALU.add)
                        v.drain().then_inc(dense_res, 1)
                with dve.Else():
                    dve.sem_inc(dense_mask, T)
                    dve.sem_inc(dense_e, T * H)
                    dve.sem_inc(dense_res, T)
                settle()

            def bridge():
                t_f = 0
                dve.wait_ge(mean_ready, 1)
                graph_terms(0)
                for u in range(T):
                    if u == LATE_AT:
                        late_lists(0, B)
                    if FINISH[u]:
                        finish_a(B - 1, t_f)
                    weights(0, u, None, None)
                    for i in range(FINISH[u]):
                        if i:
                            finish_a(B - 1, t_f)
                        finish_b(B - 1, t_f)
                        t_f += 1
                    attend(0, u, None, None)
                    if u == 0:
                        redo(B - 1)
                    if u == SORT_AT:
                        early_lists(1, B + 1)

            def stage2(b, reduce, finish):
                t_f = 0
                if reduce:
                    graph_terms(b)
                if isinstance(b, int) and b == B:
                    settle()
                combine(b - 1, T - 1)
                settle()
                dense(b - 1)
                rb = b if reduce else None
                for u in range(T):
                    if reduce and u == LATE_AT:
                        late_lists(b, B + b)
                    if FINISH[u] and not t_f:
                        wait_pair(b - 1, 0)
                        settle()
                        variance(pair[0][:, 0:C], 0)
                        v.drain().then_inc(var_ready, 1)
                    weights(rb, u, b - 1, t_f if FINISH[u] else None)
                    attend(rb, u, b - 1, t_f if FINISH[u] else None)
                    if FINISH[u]:
                        t_f += 1
                    for _ in range(1, FINISH[u]):
                        weights(None, u, b - 1, t_f)
                        attend(None, u, b - 1, t_f)
                        t_f += 1
                    if reduce and u == SORT_AT and not (isinstance(b, int) and b == B - 1):
                        early_lists(b + 1, B + b + 1)
                last_norm(b - 1)

            program(dve, stage1, bridge, stage2)


_INS = ["x", "adj", "L0_gnn_W", "L0_gnn_b", "L1_gnn_W", "L1_gnn_a1", "L1_gnn_a2",
        "L1_gnn_edge_emb", "L1_gnn_ln_gamma", "L1_gnn_ln_beta"]


def kernel(**inputs):
    import numpy as _np
    import concourse.bacc as _bacc
    from concourse import mybir as _mybir
    from concourse.bass_utils import run_bass_kernel_spmd as _run

    nc = _bacc.Bacc("TRN2", target_bir_lowering=False, num_devices=1)
    arrays, args = {}, []
    for name in _INS:
        a = _np.ascontiguousarray(inputs[name])
        arrays[f"in_{name}_dram"] = a
        args.append(nc.dram_tensor(f"in_{name}_dram", a.shape, _mybir.dt.from_np(a.dtype),
                                   kind="ExternalInput").ap())
    out = nc.dram_tensor("out_dram", (B, N, C), _mybir.dt.float32, kind="ExternalOutput").ap()
    build(nc, *args, out)
    r = _run(nc, [arrays], core_ids=[0])
    return r.results[0]["out_dram"]
```

```python
import numpy as np
import concourse.bass as bass
from concourse import mybir
from contextlib import ExitStack

F32 = mybir.dt.float32
BF16 = mybir.dt.bfloat16
I32 = mybir.dt.int32
ALU = mybir.AluOpType
ACT = mybir.ActivationFunctionType
AX = mybir.AxisListType.X

P = 128
B, N, C = 8, 2048, 256
H, DH = 8, 32
T = N // P
TOP = 25
PART = 13
LIST = 32
CH = N // 16
CAND = 16 * 8
ROW = C + H
MARK = 4096.0
FAR = -1.0e30
LOWEST = -3.0e38
EPS = 1e-5
SLOTS = [25, 19, 17, 15, 14, 13, 13, 12, 12, 11, 11, 10, 10, 9, 8, 8]
SEARCH = [3, 2, 2, 2, 1, 1, 1, 1, 1, 1, 1, 0, 0, 0, 0, 0]
FINISH = [0, 1, 1, 1, 1, 1, 1, 1, 1, 1, 1, 1, 1, 1, 1, 2]


def ahead(b, u, lead, search, more):
    begun = 0 if isinstance(b, int) and b == -1 else lead
    done = min(sum(SEARCH[:u]) + lead, T) if u else begun
    here = range(done, min(sum(SEARCH[:u + 1]) + lead, T)) if search else []
    then = range(lead) if more and u == SORT_AT + 1 else []
    return [(b + 1, t) for t in here] + [(b + 2, t) for t in then]


CONSTS = 22 + T
SCORE_CONSTS = 8
RING = sum(SLOTS[:3])
RING_AT = [0, 25, 44, 0, 15, 29, 42, 0, 12, 24, 35, 46, 0, 10, 45, 53]
BACK = [3, 4, 3, 3, 3, 4, 4, 4, 4, 4, 4, 4, 4, 4, 3, 4]
SORT_AT = 10
LATE_AT = 3
LAG = 3


def build(nc, x, adj, w0, b0, w1, a1, a2, emb, gamma, beta, out):
    ctx = ExitStack()
    with ctx:
        def sb(name, shape, dt=F32):
            return ctx.enter_context(nc.sbuf_tensor(name, shape, dt))

        def pb(name, shape):
            return ctx.enter_context(nc.psum_tensor(name, shape, F32))

        def sem(name):
            return ctx.enter_context(nc.semaphore(name))

        def dram(name, width):
            return nc.dram_tensor(name, (B * N, width), F32).ap()

        agg_d = dram("agg_d", C)
        x1_d = dram("x1_d", C)
        table_d = dram("table_d", ROW)
        first_d = nc.dram_tensor("first_d", (N, ROW), F32).ap()
        att_d = dram("att_d", C)

        x_rows = x.rearrange("b n c -> (b n) c")
        adj_rows = adj.rearrange("b n m -> (b n) m")
        out_rows = out.rearrange("b n c -> (b n) c")

        adj_i = [sb(f"adj_i{q}", [P, N], I32) for q in range(2)]
        adj_h2 = sb("adj_h2", [P, 2 * N], BF16)
        adj_h = [adj_h2[:, N * q:N * (q + 1)] for q in range(2)]
        cand = sb("cand", [P, CAND])
        lists = sb("lists", [P, T * LIST])
        eighth = sb("eighth", [P, T])
        degree = sb("degree", [P, B * T])
        key = sb("key", [P, T])
        key2 = sb("key2", [P, T])
        order = sb("order", [P, T])
        picks = sb("picks", [P, B * T * T])
        wide = sb("wide", [P, T * ROW])
        moved = sb("moved", [P, T * LIST])
        fill = sb("fill", [P, T * LIST])
        small = sb("small", [P, T * T])
        tile_of = sb("tile_of", [P, T])
        own = sb("own", [P, T])
        idx_all = sb("idx_all", [P, B * T * LIST], I32)
        own_all = sb("own_all", [P, B * T], I32)
        deg_all = sb("deg_all", [P, B * T])
        low_all = sb("low_all", [P, B * T])
        has_all = sb("has_all", [P, B * T])
        hasnt_all = sb("hasnt_all", [P, B * T])
        idx_cur = sb("idx_cur", [P, T * LIST], I32)
        own_cur = sb("own_cur", [P, T], I32)
        flag_in = sb("flag_in", [P, 2])
        flag_i = sb("flag_i", [1, 2 * B], I32)
        ring = sb("ring", [P, RING * ROW])
        res = [sb(f"res{q}", [P, C]) for q in range(4)]
        pair = [sb(f"pair{q}", [P, 2 * C]) for q in range(2)]
        h_t = sb("h_t", [P, 2 * C])
        y = sb("y", [P, C])
        z = sb("z", [P, C])
        stats = sb("stats", [P, 12])
        mv = sb("mv", [P, 4])
        var = sb("var", [P, 2])
        std = sb("std", [P, 2])
        rstd = sb("rstd", [P, 2])
        y2 = sb("y2", [P, C])
        x1 = [sb(f"x1{q}", [P, C]) for q in range(2)]
        x1_t = sb("x1_t", [P, C])
        tab = [sb(f"tab{q}", [P, ROW]) for q in range(2)]
        self_s = sb("self_s", [P, B * T * H])
        mean_wh = sb("mean_wh", [P, B * C])
        self_cur = sb("self_cur", [P, T * H])
        far_cur = sb("far_cur", [P, T * LIST])
        e = sb("e", [P, LIST * H])
        pr = sb("pr", [P, LIST * H])
        mx = sb("mx", [P, H])
        su = sb("su", [P, H])
        neg = sb("neg", [P, C])
        w0_s = sb("w0_s", [P, 4, C])
        w1_s = sb("w1_s", [P, 2, ROW + H])
        b0_s = sb("b0_s", [1, C])
        b1_s = sb("b1_s", [1, ROW + H])
        a1_s = sb("a1_s", [P, DH])
        a2_s = sb("a2_s", [P, DH])
        gam = sb("gam", [P, C])
        bet = sb("bet", [P, C])
        ident = sb("ident", [P, P])
        mark_h = sb("mark_h", [P, P], BF16)
        ones_h = sb("ones_h", [64, P], BF16)
        value_row = sb("value_row", [P, N])
        cols_h = sb("cols_h", [64, N], BF16)
        ones = sb("ones", [P, P])
        c_i = sb("c_i", [P, 64], I32)
        rev = sb("rev", [P, T])
        tno = sb("tno", [P, T])
        kno = sb("kno", [P, LIST])
        row_p = sb("row_p", [P, 1])
        base_b = sb("base_b", [P, B])
        slots_c = sb("slots_c", [P, T])
        all_idx = sb("all_idx", [P, LIST], I32)
        all_own = sb("all_own", [P, 1], I32)
        all_res = sb("all_res", [P, C])
        top = sb("top", [P, LIST])
        sums = sb("sums", [P, H])
        lone = sb("lone", [P, 2])
        peak = sb("peak", [P, 1])
        cols_i = wide[:, N:2 * N].bitcast(I32)
        all_g = wide[:, 0:PART * C]
        mask = adj_i[1][:, :].bitcast(F32)
        heat = adj_h2[:, :].bitcast(F32)
        graph_tab = wide[:, :]
        heat_t = adj_i[0][:, :].bitcast(F32)

        score_p = [pb(f"score_p{h}", [P, N // 2]) for h in range(2)]
        turn_p = pb("turn_p", [P, 2 * C])
        lin_p = pb("lin_p", [P, 2 * C])
        wh_p = pb("wh_p", [P, 2 * C])
        sum_p = pb("sum_p", [P, 2 * C])

        att_p = [score_p[q][:, 0:C] for q in range(2)]

        passed = sem("passed")
        weights_ld = sem("weights_ld")
        consts_done = sem("consts_done")
        weights_done = sem("weights_done")
        adj_ld = [sem(f"adj_ld{q}") for q in range(2)]
        cast_done = sem("cast_done")
        score_ready = sem("score_ready")
        score_used = sem("score_used")
        flag_put = sem("flag_put")
        flag_summed = sem("flag_summed")
        flag_ready = sem("flag_ready")
        again_dma = sem("again_dma")
        again_ld = sem("again_ld")
        again_used = sem("again_used")
        early_ready = sem("early_ready")
        late_ready = sem("late_ready")
        rows_ld = [sem(f"rows_ld{q}") for q in range(4)]
        rows_used0 = sem("rows_used0")
        rows_used = sem("rows_used")
        res_ready = sem("res_ready")
        res_out = [sem(f"res_out{q}") for q in range(4)]
        graph_out = sem("graph_out")
        redo_idx = sem("redo_idx")
        redo_dma = sem("redo_dma")
        redo_ld = sem("redo_ld")
        redo_res = sem("redo_res")
        redo_out = sem("redo_out")
        dense_go = sem("dense_go")
        dense_dma = sem("dense_dma")
        dense_tab = sem("dense_tab")
        dense_adj = sem("dense_adj")
        dense_mask = sem("dense_mask")
        dense_row = sem("dense_row")
        dense_e = sem("dense_e")
        dense_p = sem("dense_p")
        dense_turn = sem("dense_turn")
        dense_pt = sem("dense_pt")
        dense_att = sem("dense_att")
        dense_res = sem("dense_res")
        dense_out = sem("dense_out")
        pair_ld = [sem(f"pair_ld{q}") for q in range(2)]
        turned = sem("turned")
        h_ready = sem("h_ready")
        lin_ready = sem("lin_ready")
        var_ready = sem("var_ready")
        std_ready = sem("std_ready")
        x1_ready = sem("x1_ready")
        x1_turned = sem("x1_turned")
        x1t_ready = sem("x1t_ready")
        wh_ready = sem("wh_ready")
        tab_ready = sem("tab_ready")
        summed = sem("summed")
        mean_ready = sem("mean_ready")
        tab_out = [sem(f"tab_out{q}") for q in range(2)]
        table_ready = sem("table_ready")
        first_out = sem("first_out")
        logits_ready = sem("logits_ready")
        rows_weighted = sem("rows_weighted")
        exp_ready = sem("exp_ready")
        norm_ready = sem("norm_ready")
        elu_ready = sem("elu_ready")
        pair_used = sem("pair_used")
        final_ready = sem("final_ready")
        final_out = [sem(f"final_out{q}") for q in range(2)]

        def need(eng, s, value):
            if not isinstance(value, int) or value > 0:
                eng.wait_ge(s, value)

        def hold(eng, s, value):
            if not isinstance(value, int):
                eng.wait_ge(s, value)
                eng.sem_inc(passed, 1)
            elif value > 0:
                eng.wait_ge(s, value)

        half, quarter, hl = T // 2, T // 4, T // 2 * LIST

        def landed(eng, dma_sem, count, to):
            eng.wait_ge(dma_sem, count)
            eng.sem_clear(dma_sem)
            eng.sem_inc(to, 1)

        def tile_at(u, width):
            return ring[:, RING_AT[u] * ROW:RING_AT[u] * ROW + SLOTS[u] * width]

        def gathered(order_b, u):
            return 16 * (order_b * sum(SLOTS[u % 4::4]) + sum(SLOTS[u % 4:u + 1:4]))

        def two_back(n, t):
            return n - 1 if t else n

        def tile_rows(b, t):
            return bass.ds(b * N + t * P, P)

        def program(eng, stage1, bridge, stage2):
            stage1(-1, True, False, False, True)
            stage1(0, True, True, False, True)
            with eng.Fori(1, B - 2) as b:
                stage1(b, True, True, True, True)
            stage1(B - 2, True, True, True, False)
            stage1(B - 1, False, True, True, False)
            bridge()
            with eng.Fori(1, B - 1) as b:
                stage2(b, True, True)
            stage2(B - 1, True, True)
            stage2(B, False, True)

        block = ctx.enter_context(nc.Block())

        @block.sync
        def _(sp):
            sp.dma_start(w0_s[:, :, :], w0.rearrange("(c p) n -> p c n", p=P)).then_inc(weights_ld, 16)
            sp.dma_start(w1_s[:, :, 0:C], w1.rearrange("(c p) n -> p c n", p=P)).then_inc(weights_ld, 16)
            sp.dma_start(b0_s[:, :], b0.rearrange("(a n) -> a n", a=1)).then_inc(weights_ld, 16)
            sp.dma_start(a1_s[:, :], a1.rearrange("(a n) -> a n", a=1).broadcast_to([P, DH])).then_inc(weights_ld, 16)
            sp.dma_start(a2_s[:, :], a2.rearrange("(a n) -> a n", a=1).broadcast_to([P, DH])).then_inc(weights_ld, 16)
            sp.dma_start(gam[:, :], gamma.rearrange("(a n) -> a n", a=1).broadcast_to([P, C])).then_inc(weights_ld, 16)
            sp.dma_start(bet[:, :], beta.rearrange("(a n) -> a n", a=1).broadcast_to([P, C])).then_inc(weights_ld, 16)
            sp.wait_ge(consts_done, 1)
            sp.dma_start(b1_s[:, ROW:ROW + H], emb[1:2, :]).then_inc(weights_ld, 16)

            def load_adj(b, t):
                n, q = b * T + t, t % 2
                need(sp, cast_done, n - 1)
                sp.dma_start(adj_i[q][:, :], adj_rows[tile_rows(b, t), :]).then_inc(adj_ld[q], 16)

            def search_again(b):
                hold(sp, flag_ready, 2 * b + 1)
                over = sp.value_load(flag_i[0:1, bass.ds(2 * b, 1)])
                with sp.If(over > 0):
                    with sp.Fori(0, T) as t:
                        sp.wait_ge(again_used, b * T + t)
                        sp.dma_start(adj_i[0][:, :], adj_rows[bass.ds(b * N + t * P, P), :])\
                            .then_inc(again_dma, 16)
                        landed(sp, again_dma, 16, again_ld)
                with sp.Else():
                    sp.sem_inc(again_ld, T)
                hold(sp, again_used, T * (b + 1))

            def load_pair(b, t):
                n, q = b * T + t, t % 2
                if t == 0:
                    hold(sp, graph_out, b + 1)
                need(sp, x1_ready, two_back(n, t))
                sp.dma_start(pair[q][:, 0:C], x_rows[tile_rows(b, t), :]).then_inc(pair_ld[q], 16)
                sp.dma_start(pair[q][:, C:2 * C], agg_d[tile_rows(b, t), :]).then_inc(pair_ld[q], 16)

            def store_table(b, t):
                n, q = b * T + t, t % 2
                sp.wait_ge(tab_ready, n + 1)
                sp.dma_start(x1_d[tile_rows(b, t), :], x1[q][:, :]).then_inc(tab_out[q], 16)
                sp.dma_start(table_d[tile_rows(b, t), :], tab[q][:, :]).then_inc(tab_out[q], 16)
                if t == T - 1:
                    for q in range(2):
                        sp.wait_ge(tab_out[q], 16 * T * (b + 1))
                    sp.sem_inc(table_ready, 1)

            def stage1(b, search, reduce, finish, more):
                t_f = 0
                for u in range(T):
                    if search and u == SORT_AT:
                        search_again(b + 1)
                    for _ in range(FINISH[u] if finish else 0):
                        if not t_f:
                            load_pair(b - 1, 0)
                        if t_f < T - 1:
                            load_pair(b - 1, t_f + 1)
                        if t_f:
                            store_table(b - 1, t_f - 1)
                        t_f += 1
                    for at in ahead(b, u, 4, search, more):
                        load_adj(*at)
                if finish:
                    store_table(b - 1, T - 1)

            def bridge():
                sp.wait_ge(table_ready, 1)
                sp.dma_start(first_d, table_d[0:N, :]).then_inc(first_out, 16)
                stage1(B, False, False, True, False)

            def dense(b):
                hold(sp, graph_out, B + b + 1)
                hold(sp, dense_go, b + 1)
                hold(sp, flag_ready, 2 * b + 2)
                many = sp.value_load(flag_i[0:1, bass.ds(2 * b + 1, 1)])
                with sp.If(many > 0):
                    sp.dma_start(graph_tab.rearrange("p (t c) -> p t c", c=ROW),
                                 table_d[bass.ds(b * N, N), :].rearrange("(t p) c -> p t c", p=P))\
                        .then_inc(dense_dma, 16)
                    landed(sp, dense_dma, 16, dense_tab)
                    with sp.Fori(0, T) as t:
                        sp.wait_ge(dense_mask, b * T + t)
                        sp.dma_start(adj_i[0][:, :], adj_rows[bass.ds(b * N + t * P, P), :])\
                            .then_inc(dense_dma, 16)
                        landed(sp, dense_dma, 16, dense_adj)
                        sp.wait_ge(dense_res, b * T + t + 1)
                        sp.dma_start(att_d[bass.ds(b * N + t * P, P), :], all_res[:, :])\
                            .then_inc(dense_dma, 16)
                        landed(sp, dense_dma, 16, dense_out)
                with sp.Else():
                    sp.sem_inc(dense_tab, 1)
                    sp.sem_inc(dense_adj, T)
                    sp.sem_inc(dense_out, T)

            def load_pair2(b, t):
                n, q = b * T + t, t % 2
                if t == 0:
                    hold(sp, graph_out, B + b + 1)
                need(sp, pair_used, two_back(n, t))
                sp.dma_start(pair[q][:, 0:C], att_d[tile_rows(b, t), :]).then_inc(pair_ld[q], 16)
                sp.dma_start(pair[q][:, C:2 * C], x1_d[tile_rows(b, t), :]).then_inc(pair_ld[q], 16)

            def store_final(b, t):
                n, q = b * T + t, t % 2
                sp.wait_ge(final_ready, n + 1)
                sp.dma_start(out_rows[tile_rows(b, t), :], x1[q][:, :]).then_inc(final_out[q], 16)

            def stage2(b, reduce, finish):
                t_f = 0
                for u in range(T):
                    for _ in range(FINISH[u] if finish else 0):
                        if not t_f:
                            dense(b - 1)
                            load_pair2(b - 1, 0)
                        if t_f < T - 1:
                            load_pair2(b - 1, t_f + 1)
                        if t_f:
                            store_final(b - 1, t_f - 1)
                        t_f += 1
                if finish:
                    store_final(b - 1, T - 1)

            program(sp, stage1, bridge, stage2)
            for q in range(2):
                sp.wait_ge(final_out[q], 16 * B * T // 2)

        @block.gpsimd
        def _(pool):
            steps = 0

            def step(last):
                nonlocal steps
                steps += 1
                last.then_inc(consts_done, 1)
                pool.wait_ge(consts_done, steps)

            step(pool.memset(b1_s[:, :], 0.0))
            step(pool.memset(mark_h[:, :], 0.0))
            step(pool.memset(ones_h[:, :], 1.0))
            step(pool.memset(cols_i[0:64, :], 0))
            step(pool.affine_select(out=mark_h[:, :], in_=mark_h[:, :], compare_op=ALU.not_equal,
                                    fill=MARK, base=0, pattern=[[-1, P]], channel_multiplier=1))
            step(pool.iota(cols_i[0:1, :], pattern=[[-8, N // 8], [0, 8]], base=N, channel_multiplier=0))
            step(pool.iota(cols_i[32:33, :], pattern=[[0, N // 8], [-1, 8]], base=0, channel_multiplier=0))
            step(pool.tensor_copy(cols_h[:, :], cols_i[0:64, :]))
            assert steps == SCORE_CONSTS
            step(pool.memset(ident[:, :], 0.0))
            step(pool.memset(ones[:, :], 1.0))
            for u in range(T):
                step(pool.memset(slots_c[:, u:u + 1], float(SLOTS[u])))
            step(pool.iota(c_i[:, 0:T], pattern=[[1, T]], base=0, channel_multiplier=0))
            step(pool.iota(c_i[:, T:T + LIST], pattern=[[1, LIST]], base=0, channel_multiplier=0))
            step(pool.iota(c_i[:, 48:49], pattern=[[0, 1]], base=0, channel_multiplier=1))
            step(pool.iota(c_i[:, 49:49 + B], pattern=[[N, B]], base=0, channel_multiplier=0))
            step(pool.affine_select(out=ident[:, :], in_=ident[:, :], compare_op=ALU.not_equal,
                                    fill=1.0, base=0, pattern=[[-1, P]], channel_multiplier=1))
            step(pool.tensor_copy(tno[:, :], c_i[:, 0:T]))
            step(pool.tensor_copy(kno[:, :], c_i[:, T:T + LIST]))
            step(pool.tensor_copy(row_p[:, :], c_i[:, 48:49]))
            step(pool.tensor_copy(base_b[:, :], c_i[:, 49:49 + B]))
            step(pool.iota(cols_i[:, :], pattern=[[-1, N]], base=int(MARK) + N, channel_multiplier=0))
            step(pool.tensor_copy(value_row[:, :], cols_i[:, :]))
            step(pool.tensor_scalar(rev[:, :], tno[:, :], -1.0, float(T - 1), ALU.mult, ALU.add))
            assert steps == CONSTS

            redone = pool.alloc_register("redone")
            pool.reg_mov(redone, 0)

            def gather(b, u, table, width, order_b):
                n, before = order_b * T + u, order_b * T + u - BACK[u] + 1
                if table is x_rows:
                    hold(pool, rows_used0, before)
                elif isinstance(order_b, int) and order_b == B and u < BACK[u]:
                    pool.wait_ge(rows_used0, before)
                else:
                    hold(pool, rows_used, before - B * T)
                for k in range(SLOTS[u]):
                    at = u * LIST + k
                    pool.indirect_dma_start(
                        out=tile_at(u, width)[:, k * width:(k + 1) * width], out_offset=None, in_=table,
                        in_offset=bass.IndirectOffsetOnAxis(ap=idx_cur[:, at:at + 1], axis=0),
                        bounds_check=B * N - 1, oob_is_err=False).then_inc(rows_ld[u % 4], 16)

            def scatter(order_b, u, to):
                n, q = order_b * T + u, u % 4
                hold(pool, res_ready, n + 1)
                pool.indirect_dma_start(
                    out=to, out_offset=bass.IndirectOffsetOnAxis(ap=own_cur[:, u:u + 1], axis=0),
                    in_=res[q][:, :], in_offset=None, bounds_check=B * N - 1,
                    oob_is_err=False).then_inc(res_out[q], 16)

            def redo(b):
                hold(pool, flag_ready, 2 * b + 2)
                many = pool.value_load(flag_i[0:1, bass.ds(2 * b + 1, 1)])
                with pool.If(many > 0):
                    for q in range(4):
                        hold(pool, res_out[q], 16 * quarter * (b + 1))
                    with pool.Fori(0, T) as u:
                        for part, slots in enumerate((range(PART), range(PART, TOP))):
                            hold(pool, redo_idx, 2 * (b * T + u) + part + 1)
                            for i, k in enumerate(slots):
                                pool.indirect_dma_start(
                                    out=all_g[:, i * C:(i + 1) * C], out_offset=None, in_=x_rows,
                                    in_offset=bass.IndirectOffsetOnAxis(ap=all_idx[:, k:k + 1], axis=0),
                                    bounds_check=B * N - 1, oob_is_err=False).then_inc(redo_dma, 16)
                            pool.reg_add(redone, redone, 16 * len(slots))
                            pool.wait_ge(redo_dma, redone)
                            pool.sem_inc(redo_ld, 1)
                        hold(pool, redo_res, b * T + u + 1)
                        pool.indirect_dma_start(
                            out=agg_d, out_offset=bass.IndirectOffsetOnAxis(ap=all_own[:, :], axis=0),
                            in_=all_res[:, :], in_offset=None, bounds_check=B * N - 1,
                            oob_is_err=False).then_inc(redo_dma, 16)
                        pool.reg_add(redone, redone, 16)
                        pool.wait_ge(redo_dma, redone)
                        pool.sem_inc(redo_out, 1)
                with pool.Else():
                    pool.sem_inc(redo_ld, 2 * T)
                    pool.sem_inc(redo_out, T)

            def end_graph(order_b):
                for q in range(4):
                    hold(pool, res_out[q], 16 * quarter * (order_b + 1))
                pool.sem_inc(graph_out, 1)

            def stage1(b, search, reduce, finish, more):
                for u in range(T if reduce else 0):
                    if u == 0:
                        hold(pool, early_ready, b + 1)
                    if u == T // 2:
                        hold(pool, late_ready, b + 1)
                    gather(b, u, x_rows, C, b)
                    if u == 0 and finish:
                        for w in range(T - LAG, T):
                            scatter(b - 1, w, agg_d)
                        redo(b - 1)
                        end_graph(b - 1)
                    if u >= LAG:
                        scatter(b, u - LAG, agg_d)

            def bridge():
                pool.wait_ge(early_ready, B + 1)
                pool.wait_ge(first_out, 16)
                gather(0, 0, first_d, ROW, B)
                for w in range(T - LAG, T):
                    scatter(B - 1, w, agg_d)
                redo(B - 1)
                end_graph(B - 1)
                for u in range(1, T):
                    if u == T // 2:
                        pool.wait_ge(late_ready, B + 1)
                    gather(0, u, first_d, ROW, B)
                    if u >= LAG:
                        scatter(B, u - LAG, att_d)

            def stage2(b, reduce, finish):
                for u in range(T if reduce else 0):
                    if u == 0:
                        hold(pool, early_ready, B + b + 1)
                        pool.wait_ge(table_ready, B)
                    if u == T // 2:
                        hold(pool, late_ready, B + b + 1)
                    gather(b, u, table_d, ROW, B + b)
                    if u == 0 and finish:
                        for w in range(T - LAG, T):
                            scatter(B + b - 1, w, att_d)
                        end_graph(B + b - 1)
                    if u >= LAG:
                        scatter(B + b, u - LAG, att_d)
                if finish and not reduce:
                    for w in range(T - LAG, T):
                        scatter(B + b - 1, w, att_d)
                    end_graph(B + b - 1)

            program(pool, stage1, bridge, stage2)

        @block.scalar
        def _(act):
            def cast(b, t):
                n, q = b * T + t, t % 2
                act.wait_ge(adj_ld[q], 16 * (b * (T // 2) + t // 2 + 1))
                need(act, score_ready, 2 * n - 2)
                act.activation(adj_h[q], adj_i[q][:, :], ACT.Copy,
                               accum_out=degree[:, bass.ds(n, 1)]).then_inc(cast_done, 1)

            def finish_a(b, t):
                n = b * T + t
                act.wait_ge(turned, n + 1)
                need(act, lin_ready, n)
                act.activation(h_t[:, :], turn_p[:, :], ACT.Copy).then_inc(h_ready, 1)

            def finish_b(b, t):
                n, q = b * T + t, t % 2
                act.wait_ge(x1_turned, n + 1)
                need(act, wh_ready, n)
                act.activation(x1_t[:, :], turn_p[:, 0:C], ACT.Copy).then_inc(x1t_ready, 1)
                act.wait_ge(wh_ready, n + 1)
                need(act, tab_out[q], 16 * (b * T + t // 2 * 2))
                need(act, summed, two_back(n, t))
                act.activation(tab[q][:, :], wh_p[:, 0:ROW], ACT.Copy)
                act.activation(self_s[:, bass.ds(n * H, H)], wh_p[:, ROW:ROW + H], ACT.Copy)\
                    .then_inc(tab_ready, 1)
                if t == T - 1:
                    act.wait_ge(summed, n + 1)
                    act.activation(mean_wh[:, bass.ds(b * C, C)], sum_p[:, 0:C], ACT.Copy,
                                   scale=1.0 / N).then_inc(mean_ready, 1)

            def root1(b, t):
                act.wait_ge(var_ready, b * T + t + 1)
                act.activation(std[:, 0:1], var[:, 0:1], ACT.Sqrt).then_inc(std_ready, 1)

            def finish(b, t):
                finish_a(b, t)
                if t:
                    finish_b(b, t - 1)
                root1(b, t)
                if t == T - 1:
                    finish_b(b, t)

            def stage1(b, search, reduce, finish_, more):
                t_f = 0
                for u in range(T):
                    for _ in range(FINISH[u] if finish_ else 0):
                        finish(b - 1, t_f)
                        t_f += 1
                    for at in ahead(b, u, 2, search, more):
                        cast(*at)

            def bridge():
                exps(0, 0)
                finish_a(B - 1, 0)
                for u in range(1, T):
                    root1(B - 1, u - 1)
                    exps(0, u)
                    finish_b(B - 1, u - 1)
                    finish_a(B - 1, u)
                root1(B - 1, T - 1)
                finish_b(B - 1, T - 1)

            def exps(b, u):
                n, w = b * T + u, SLOTS[u] * H
                act.wait_ge(logits_ready, n + 1)
                act.activation(pr[:, 0:w], e[:, 0:w], ACT.Exp).then_inc(exp_ready, 1)

            def elu(b, t):
                n = b * T + t
                act.wait_ge(norm_ready, n + 1)
                act.activation(neg[:, :], z[:, :], ACT.Relu, scale=-1.0)
                act.drain()
                act.activation(neg[:, :], neg[:, :], ACT.Exp, scale=-1.0).then_inc(elu_ready, 1)

            def root(b, j):
                act.wait_ge(var_ready, B * T + b * (T + 1) + j + 1)
                act.activation(std[:, :], var[:, :], ACT.Sqrt).then_inc(std_ready, 1)

            def dense(b):
                hold(act, dense_out, T * b)
                act.wait_ge(flag_ready, 2 * b + 2)
                many = act.value_load(flag_i[0:1, bass.ds(2 * b + 1, 1)])
                with act.If(many > 0):
                    with act.Fori(0, T) as t:
                        with act.Fori(0, H) as h:
                            m = (b * T + t) * H + h
                            act.wait_ge(dense_res, b * T + t)
                            act.wait_ge(dense_e, m + 1)
                            act.activation(heat, heat, ACT.Exp, bias=peak[:, 0:1],
                                           accum_out=sums[:, bass.ds(h, 1)]).then_inc(dense_p, 1)
                            act.wait_ge(dense_att, m)
                            for g in range(4):
                                act.wait_ge(dense_turn, 4 * m + g + 1)
                                act.activation(heat_t[:, 512 * g:512 * (g + 1)], turn_p[:, :],
                                               ACT.Copy).then_inc(dense_pt, 1)
                with act.Else():
                    act.sem_inc(dense_p, T * H)
                    act.sem_inc(dense_pt, 4 * T * H)

            def stage2(b, reduce, finish):
                t_f = 0
                dense(b - 1)
                for u in range(T):
                    if FINISH[u] and not t_f:
                        root(b - 1, 0)
                    if reduce:
                        exps(b, u)
                    for _ in range(FINISH[u]):
                        elu(b - 1, t_f)
                        t_f += 1
                        root(b - 1, t_f)

            program(act, stage1, bridge, stage2)

        @block.tensor
        def _(pe):
            pe.wait_ge(consts_done, SCORE_CONSTS)

            def scores(b, t):
                n, q = b * T + t, t % 2
                pe.wait_ge(cast_done, n + 1)
                for h in range(2):
                    need(pe, score_used, 2 * n + h - 1)
                    for c in range(2):
                        o = score_p[h][:, 512 * c:512 * (c + 1)]
                        at = slice(1024 * h + 512 * c, 1024 * h + 512 * (c + 1))
                        pe.matmul(o, mark_h[:, :], adj_h[q][:, at], start=True, stop=False)
                        last = pe.matmul(o, ones_h[:, :], cols_h[:, at], start=False, stop=True)
                    last.then_inc(score_ready, 1)

            def sum_flag(k, col):
                pe.wait_ge(flag_put, k)
                pe.matmul(wh_p[0:1, 2 * C - 2 + col:2 * C - 1 + col], ones[:, 0:1],
                          flag_in[:, col:col + 1], start=True, stop=True).then_inc(flag_summed, 1)
                pe.wait_ge(flag_ready, k)

            def finish_a(b, t):
                n, q = b * T + t, t % 2
                pe.wait_ge(pair_ld[q], 16 * (b * T + t // 2 * 2 + 2))
                need(pe, x1t_ready, n - 1 if t > 1 else b * T)
                for c in range(4):
                    last = pe.transpose(turn_p[:, P * c:P * (c + 1)], pair[q][:, P * c:P * (c + 1)],
                                        ident[:, :])
                last.then_inc(turned, 1)
                pe.wait_ge(h_ready, n + 1)
                need(pe, x1_ready, n)
                pe.matmul(lin_p[:, 0:C], ones[0:1, :], b0_s[0:1, :], start=True, stop=False)
                for c in range(4):
                    last = pe.matmul(lin_p[:, 0:C], h_t[:, P * c:P * (c + 1)], w0_s[:, c, :],
                                     start=False, stop=(c == 3))
                last.then_inc(lin_ready, 1)

            def finish_b(b, t):
                n, q = b * T + t, t % 2
                pe.wait_ge(x1_ready, n + 1)
                for c in range(2):
                    last = pe.transpose(turn_p[:, P * c:P * (c + 1)], x1[q][:, P * c:P * (c + 1)],
                                        ident[:, :])
                last.then_inc(x1_turned, 1)
                pe.wait_ge(x1t_ready, n + 1)
                need(pe, tab_ready, n)
                pe.matmul(wh_p[:, 0:ROW + H], ones[0:1, :], b1_s[0:1, :], start=True, stop=False)
                for c in range(2):
                    last = pe.matmul(wh_p[:, 0:ROW + H], x1_t[:, P * c:P * (c + 1)], w1_s[:, c, :],
                                     start=False, stop=(c == 1))
                last.then_inc(wh_ready, 1)
                pe.wait_ge(tab_ready, n + 1)
                if t == 0:
                    need(pe, mean_ready, b)
                pe.matmul(sum_p[:, 0:C], ones[:, :], tab[q][:, 0:C], start=(t == 0),
                          stop=(t == T - 1)).then_inc(summed, 1)

            def finish(b, t):
                finish_a(b, t)
                if t:
                    finish_b(b, t - 1)
                if t == T - 1:
                    finish_b(b, t)

            def attend(b, u):
                n, q = (B + b) * T + u, u % 2
                pe.wait_ge(rows_weighted, b * T + u + 1)
                need(pe, res_ready, n - 1)
                for k in range(SLOTS[u]):
                    last = pe.matmul(att_p[q], ident[:, :], tile_at(u, ROW)[:, k * ROW:k * ROW + C],
                                     start=(k == 0), stop=(k == SLOTS[u] - 1))
                last.then_inc(rows_used, 1)

            def stage1(b, search, reduce, finish_, more):
                t_f = 0
                begin = isinstance(b, int) and b == -1
                for u in range(T):
                    for _ in range(FINISH[u] if finish_ else 0):
                        finish(b - 1, t_f)
                        t_f += 1
                    if search and u == SORT_AT:
                        if begin:
                            pe.wait_ge(consts_done, CONSTS)
                        sum_flag(2 * b + 3, 0)
                    if search and u == SORT_AT + 1:
                        sum_flag(2 * b + 4, 1)
                    for at in ahead(b, u, 1, search, more):
                        scores(*at)
                if begin:
                    pe.wait_ge(weights_ld, 16 * 8)
                    pe.wait_ge(weights_done, 1)

            def bridge():
                attend(0, 0)
                finish_a(B - 1, 0)
                for u in range(1, T):
                    finish_b(B - 1, u - 1)
                    finish_a(B - 1, u)
                    attend(0, u)
                finish_b(B - 1, T - 1)

            def dense(b):
                hold(pe, dense_out, T * b)
                pe.wait_ge(flag_ready, 2 * b + 2)
                many = pe.value_load(flag_i[0:1, bass.ds(2 * b + 1, 1)])
                with pe.If(many > 0):
                    hold(pe, dense_tab, b + 1)
                    with pe.Fori(0, T) as t:
                        for h in range(H):
                            m = (b * T + t) * H + h
                            pe.wait_ge(dense_e, m)
                            for c in range(T):
                                last = pe.matmul(
                                    score_p[c // 8][:, P * (c % 8):P * (c % 8 + 1)],
                                    graph_tab[:, c * ROW + C + h:c * ROW + C + h + 1].broadcast_to([P, P]),
                                    ident[:, :], start=True, stop=True)
                            last.then_inc(dense_row, 1)
                            pe.wait_ge(dense_p, m + 1)
                            for g in range(4):
                                pe.wait_ge(dense_pt, 4 * m + g)
                                for c in range(4 * g, 4 * g + 4):
                                    last = pe.transpose(turn_p[:, P * (c % 4):P * (c % 4 + 1)],
                                                        heat[:, P * c:P * (c + 1)], ident[:, :])
                                last.then_inc(dense_turn, 1)
                            pe.wait_ge(dense_pt, 4 * m + 4)
                            pe.wait_ge(dense_res, b * T + t)
                            for c in range(T):
                                last = pe.matmul(sum_p[:, h * DH:(h + 1) * DH],
                                                 heat_t[:, P * c:P * (c + 1)],
                                                 graph_tab[:, c * ROW + h * DH:c * ROW + (h + 1) * DH],
                                                 start=(c == 0), stop=(c == T - 1))
                            last.then_inc(dense_att, 1)
                with pe.Else():
                    pe.sem_inc(dense_row, T * H)
                    pe.sem_inc(dense_turn, 4 * T * H)
                    pe.sem_inc(dense_att, T * H)

            def stage2(b, reduce, finish_):
                dense(b - 1)
                for u in range(T if reduce else 0):
                    attend(b, u)

            program(pe, stage1, bridge, stage2)

        @block.vector
        def _(dve):
            v = nc.vector

            def settle():
                v.drain()

            v.memset(var[:, :], 1.0)
            v.memset(moved[:, :], 0.0)

            def score_weights():
                dve.wait_ge(weights_ld, 16 * 8)
                for a_s, to in ((a2_s, C), (a1_s, ROW)):
                    settle()
                    for c in range(2):
                        prod = wide[:, C * c:C * (c + 1)].rearrange("p (h d) -> p h d", d=DH)
                        v.tensor_tensor(prod, w1_s[:, c, 0:C].rearrange("p (h d) -> p h d", d=DH),
                                        a_s[:, :].unsqueeze(1).broadcast_to([P, H, DH]), ALU.mult)
                    settle()
                    for c in range(2):
                        prod = wide[:, C * c:C * (c + 1)].rearrange("p (h d) -> p h d", d=DH)
                        v.tensor_reduce(w1_s[:, c, to:to + H], prod, AX, ALU.add)
                v.drain().then_inc(weights_done, 1)

            def top_lists(src, put):
                for r in range(4):
                    v.max(put(r), src)
                    settle()
                    if r < 3:
                        v.match_replace(src, put(r), src, 0.0)
                        settle()

            def search(b, t):
                n = b * T + t
                settle()
                for h in range(2):
                    hold(dve, score_ready, 2 * n + h + 1)
                    for c in range(8):
                        at = 8 * (8 * h + c)
                        last = v.max(cand[:, at:at + 8], score_p[h][:, CH * c:CH * (c + 1)])
                    last.then_inc(score_used, 1)
                settle()
                v.tensor_reduce(eighth[:, t:t + 1],
                                cand[:, :].rearrange("p (c k) -> p c k", k=8)[:, :, 7], AX, ALU.max)
                settle()
                top_lists(cand[:, :], lambda r: lists[:, t * LIST + 8 * r:t * LIST + 8 * r + 8])

            def search_again(b):
                settle()
                v.tensor_reduce(flag_in[:, 1:2], eighth[:, :], AX, ALU.max)
                settle()
                v.tensor_scalar(flag_in[:, 0:1], flag_in[:, 1:2], MARK, None, ALU.is_gt)\
                    .then_inc(flag_put, 1)
                hold(dve, flag_summed, 2 * b + 1)
                v.tensor_copy(flag_i[0:1, bass.ds(2 * b, 1)], wh_p[0:1, 2 * C - 2:2 * C - 1])\
                    .then_inc(flag_ready, 1)
                hold(dve, flag_ready, 2 * b + 1)
                over = dve.value_load(flag_i[0:1, bass.ds(2 * b, 1)])
                with dve.If(over > 0):
                    with dve.Fori(0, T) as t:
                        dve.wait_ge(again_ld, b * T + t + 1)
                        v.tensor_tensor(wide[:, 0:N], adj_i[0][:, :], value_row[:, :], ALU.mult)\
                            .then_inc(again_used, 1)
                        settle()
                        top_lists(wide[:, 0:N], lambda r: top[:, 8 * r:8 * r + 8])
                        settle()
                        v.tensor_copy(lists[:, bass.ds(t * LIST, LIST)], top[:, :])
                        settle()
                with dve.Else():
                    dve.sem_inc(again_used, T)

            def sort(b):
                at, cur = bass.ds(b * T, T), bass.ds(b * T * LIST, T * LIST)
                v.scalar_tensor_tensor(key[:, :], degree[:, at], float(T), rev[:, :],
                                       ALU.mult, ALU.add)
                settle()
                v.max(order[:, 0:8], key[:, :])
                settle()
                v.match_replace(key2[:, :], order[:, 0:8], key[:, :], -1.0)
                settle()
                v.max(order[:, 8:16], key2[:, :])
                settle()
                pick = picks[:, bass.ds(b * T * T, T * T)].rearrange("p (u t) -> p u t", t=T)
                v.tensor_tensor(pick, order[:, :].unsqueeze(2).broadcast_to([P, T, T]),
                                key[:, :].unsqueeze(1).broadcast_to([P, T, T]), ALU.is_equal)
                settle()
                for i in range(2):
                    prod = wide[:, 0:half * TOP * T].rearrange("p (u k t) -> p u k t", k=TOP, t=T)
                    v.tensor_tensor(prod, pick[:, half * i:half * (i + 1), :].unsqueeze(2)
                                    .broadcast_to([P, half, TOP, T]),
                                    lists[:, :].rearrange("p (t k) -> p k t", k=LIST)[:, 0:TOP, :]
                                    .unsqueeze(1).broadcast_to([P, half, TOP, T]), ALU.mult)
                    settle()
                    v.tensor_reduce(moved[:, hl * i:hl * (i + 1)]
                                    .rearrange("p (u k) -> p u k", k=LIST)[:, :, 0:TOP],
                                    prod, AX, ALU.add)
                    settle()
                prod2 = small[:, :].rearrange("p (u t) -> p u t", t=T)
                v.tensor_tensor(prod2, pick, tno[:, :].unsqueeze(1).broadcast_to([P, T, T]), ALU.mult)
                settle()
                v.tensor_reduce(tile_of[:, :], prod2, AX, ALU.add)
                settle()
                first = moved[:, :].rearrange("p (u k) -> p u k", k=LIST)[:, :, 0:1]\
                    .broadcast_to([P, T, LIST])
                m3 = moved[:, :].rearrange("p (u k) -> p u k", k=LIST)
                v.scalar_tensor_tensor(fill[:, :].rearrange("p (u k) -> p u k", k=LIST), m3, MARK,
                                       first, ALU.is_le, ALU.mult)
                v.tensor_tensor(order[:, :], order[:, :], tile_of[:, :], ALU.add)
                v.tensor_scalar(own[:, :], tile_of[:, :], float(P), row_p[:, 0:1], ALU.mult, ALU.add)
                settle()
                v.scalar_tensor_tensor(moved[:, :], moved[:, :], MARK, moved[:, :],
                                       ALU.is_gt, ALU.mult)
                v.tensor_scalar(deg_all[:, at], order[:, :], float(T - 1), 1.0 / T,
                                ALU.subtract, ALU.mult)
                v.tensor_scalar(own_all[:, at], own[:, :], base_b[:, bass.ds(b, 1)], None, ALU.add)
                settle()
                v.tensor_tensor(moved[:, :], moved[:, :], fill[:, :], ALU.add)
                v.tensor_scalar(low_all[:, at], deg_all[:, at], float(TOP), LOWEST, ALU.is_gt, ALU.mult)
                v.tensor_scalar(has_all[:, at], deg_all[:, at], 0.5, None, ALU.is_gt)
                v.tensor_scalar(hasnt_all[:, at], deg_all[:, at], 0.5, None, ALU.is_lt)
                v.tensor_tensor(key[:, :], deg_all[:, at], slots_c[:, :], ALU.subtract)
                settle()
                v.tensor_scalar(moved[:, :], moved[:, :], -1.0, MARK + N, ALU.mult, ALU.add)
                v.tensor_reduce(key2[:, 0:1], key[:, :], AX, ALU.max)
                settle()
                v.tensor_scalar(idx_all[:, cur], moved[:, :], float(N - 1), base_b[:, bass.ds(b, 1)],
                                ALU.min, ALU.add)
                v.tensor_scalar(flag_in[:, 1:2], key2[:, 0:1], 0.0, None, ALU.is_gt)\
                    .then_inc(flag_put, 1)

            def many_flag(b):
                hold(dve, flag_summed, 2 * b + 2)
                v.tensor_copy(flag_i[0:1, bass.ds(2 * b + 1, 1)], wh_p[0:1, 2 * C - 1:2 * C])\
                    .then_inc(flag_ready, 1)

            def early_lists(b, order_b):
                settle()
                hold(dve, rows_ld[(half - 1) % 4], gathered(order_b - 1, half - 1))
                for q in range(4):
                    hold(dve, res_out[q], 16 * ((order_b - 1) * quarter + quarter // 2))
                v.tensor_copy(idx_cur[:, 0:hl], idx_all[:, bass.ds(b * T * LIST, hl)])
                v.tensor_copy(own_cur[:, 0:half], own_all[:, bass.ds(b * T, half)]).then_inc(early_ready, 1)

            def late_lists(b, order_b):
                for q in range(4):
                    hold(dve, res_out[q], 16 * (order_b * quarter))
                v.tensor_copy(idx_cur[:, hl:2 * hl], idx_all[:, bass.ds(b * T * LIST + hl, hl)])
                v.tensor_copy(own_cur[:, half:T], own_all[:, bass.ds(b * T + half, half)])\
                    .then_inc(late_ready, 1)

            def wait_rows(order_b, u):
                dve.wait_ge(rows_ld[u % 4], gathered(order_b, u))

            def max_tile(b, u):
                n, q = b * T + u, u % 4
                settle()
                wait_rows(b, u)
                v.tensor_reduce(y[:, :], tile_at(u, C).rearrange("p (k c) -> p c k", c=C),
                                AX, ALU.max).then_inc(rows_used0, 1)
                hold(dve, res_out[q], 16 * (b * quarter + u // 4))
                settle()
                v.tensor_scalar(res[q][:, :], y[:, :], low_all[:, bass.ds(n, 1)],
                                has_all[:, bass.ds(n, 1)], ALU.max, ALU.mult).then_inc(res_ready, 1)

            def variance(src, j, last=None):
                v.bn_stats(stats[:, 6 * j:6 * j + 6], src)
                settle()
                v.bn_aggr(mv[:, 2 * j:2 * j + 2], stats[:, 6 * j:6 * j + 6])
                settle()
                return v.tensor_scalar(var[:, j:j + 1], mv[:, 2 * j + 1:2 * j + 2], EPS, None, ALU.add)

            def normal(dst, src, j):
                return v.tensor_scalar(dst, src, mv[:, 2 * j:2 * j + 1], rstd[:, j:j + 1],
                                       ALU.subtract, ALU.mult)

            def finish_a(b, t):
                n, q = b * T + t, t % 2
                settle()
                hold(dve, lin_ready, n + 1)
                v.scalar_tensor_tensor(z[:, :], lin_p[:, 0:C], 0.0, pair[q][:, 0:C], ALU.max, ALU.add)
                settle()
                variance(z[:, :], 0).then_inc(var_ready, 1)

            def finish_b(b, t):
                n, q = b * T + t, t % 2
                dve.wait_ge(std_ready, n + 1)
                v.reciprocal(rstd[:, 0:1], std[:, 0:1])
                hold(dve, tab_out[q], 16 * (b * T + t // 2 * 2))
                settle()
                hold(dve, x1_turned, two_back(n, t))
                normal(x1[q][:, :], z[:, :], 0).then_inc(x1_ready, 1)

            def redo(b):
                settle()
                hold(dve, redo_out, T * b)
                hold(dve, flag_ready, 2 * b + 2)
                many = dve.value_load(flag_i[0:1, bass.ds(2 * b + 1, 1)])
                with dve.If(many > 0):
                    with dve.Fori(0, T) as u:
                        n = b * T + u
                        hold(dve, redo_out, n)
                        v.tensor_copy(all_idx[:, :], idx_all[:, bass.ds(n * LIST, LIST)])
                        v.tensor_copy(all_own[:, :], own_all[:, bass.ds(n, 1)])
                        v.drain().then_inc(redo_idx, 1)
                        hold(dve, redo_ld, 2 * n + 1)
                        v.tensor_reduce(y[:, :], all_g.rearrange("p (k c) -> p c k", c=C),
                                        AX, ALU.max)
                        v.drain().then_inc(redo_idx, 1)
                        hold(dve, redo_ld, 2 * n + 2)
                        v.tensor_reduce(y2[:, :], all_g[:, 0:(TOP - PART) * C]
                                        .rearrange("p (k c) -> p c k", c=C), AX, ALU.max)
                        settle()
                        v.tensor_tensor(y[:, :], y[:, :], y2[:, :], ALU.max)
                        settle()
                        v.tensor_scalar(all_res[:, :], y[:, :], low_all[:, bass.ds(n, 1)],
                                        has_all[:, bass.ds(n, 1)], ALU.max, ALU.mult)
                        v.drain().then_inc(redo_res, 1)
                with dve.Else():
                    dve.sem_inc(redo_idx, 2 * T)
                    dve.sem_inc(redo_res, T)
                settle()

            def stage1(b, search_, reduce, finish, more):
                t_s = t_f = 0
                for u in range(T):
                    if reduce and u == LATE_AT:
                        late_lists(b, b)
                    if reduce and u:
                        max_tile(b, u)
                    f = FINISH[u] if finish else 0
                    if f:
                        finish_a(b - 1, t_f)
                    for _ in range(SEARCH[u] if search_ else 0):
                        search(b + 1, t_s)
                        t_s += 1
                    if reduce and not u:
                        max_tile(b, u)
                    if finish and u == 0:
                        redo(b - 1)
                    for i in range(f):
                        if i:
                            finish_a(b - 1, t_f)
                        finish_b(b - 1, t_f)
                        t_f += 1
                    if search_ and u == SORT_AT:
                        if isinstance(b, int) and b == -1:
                            dve.wait_ge(consts_done, CONSTS)
                        search_again(b + 1)
                        sort(b + 1)
                        settle()
                        early_lists(b + 1, b + 1)
                    if search_ and u == SORT_AT + 1:
                        many_flag(b + 1)
                    if u == SORT_AT and reduce and not search_:
                        early_lists(0, B)
                if isinstance(b, int) and b == -1:
                    score_weights()

            def graph_terms(b):
                settle()
                prod = wide[:, 0:T * H * T].rearrange("p (u h t) -> p u h t", h=H, t=T)
                pick = picks[:, bass.ds(b * T * T, T * T)].rearrange("p (u t) -> p u t", t=T)
                v.tensor_tensor(prod, pick.unsqueeze(2).broadcast_to([P, T, H, T]),
                                self_s[:, bass.ds(b * T * H, T * H)]
                                .rearrange("p (t h) -> p h t", h=H).unsqueeze(1)
                                .broadcast_to([P, T, H, T]), ALU.mult)
                v.tensor_tensor(far_cur[:, :].rearrange("p (u k) -> p u k", k=LIST),
                                kno[:, :].unsqueeze(1).broadcast_to([P, T, LIST]),
                                deg_all[:, bass.ds(b * T, T)].unsqueeze(2).broadcast_to([P, T, LIST]),
                                ALU.is_ge)
                settle()
                v.tensor_reduce(self_cur[:, :], wide[:, 0:T * H * T].rearrange("p (a t) -> p a t", t=T),
                                AX, ALU.add)
                v.tensor_scalar(far_cur[:, :], far_cur[:, :], FAR, None, ALU.mult)
                settle()

            def weights(b, u, fb, ft):
                q, k = u % 2, SLOTS[u]
                g3 = tile_at(u, ROW).rearrange("p (k c) -> p k c", c=ROW)
                e3 = e[:, 0:k * H].rearrange("p (k h) -> p k h", h=H)
                item = ft is not None
                settle()
                if item:
                    hold(dve, std_ready, B * T + fb * (T + 1) + ft + 1)
                    v.reciprocal(rstd[:, :], std[:, :])
                if b is not None:
                    wait_rows(B + b, u)
                    v.tensor_tensor(e3, g3[:, :, C:ROW], self_cur[:, u * H:(u + 1) * H].unsqueeze(1)
                                    .broadcast_to([P, k, H]), ALU.add)
                if item and ft:
                    hold(dve, final_out[1 - ft % 2], 16 * (fb * half + (ft - 1) // 2))
                settle()
                if b is not None:
                    v.scalar_tensor_tensor(e[:, 0:k * H], e[:, 0:k * H], 0.2, e[:, 0:k * H],
                                           ALU.mult, ALU.max)
                if item:
                    normal(z[:, :], pair[ft % 2][:, 0:C], 0)
                    if ft:
                        normal(x1[1 - ft % 2][:, :], y2[:, :], 1).then_inc(final_ready, 1)
                settle()
                if b is not None:
                    v.tensor_tensor(e3, e3, far_cur[:, u * LIST:u * LIST + k].unsqueeze(2)
                                    .broadcast_to([P, k, H]), ALU.add)
                if item:
                    v.tensor_tensor(z[:, :], z[:, :], gam[:, :], ALU.mult)
                settle()
                if b is not None:
                    v.tensor_reduce(mx[:, :], e3.rearrange("p k h -> p h k"), AX, ALU.max)
                if item:
                    v.tensor_tensor(z[:, :], z[:, :], bet[:, :], ALU.add).then_inc(norm_ready, 1)
                if b is not None:
                    settle()
                    v.tensor_tensor(e3, e3, mx[:, :].unsqueeze(1).broadcast_to([P, k, H]),
                                    ALU.subtract).then_inc(logits_ready, 1)

            def combine(b, u):
                n, q = b * T + u, u % 4
                hold(dve, res_out[q], 16 * ((B + b) * quarter + u // 4))
                hold(dve, rows_used, n + 1)
                v.scalar_tensor_tensor(res[q][:, :], mean_wh[:, bass.ds(b * C, C)],
                                       hasnt_all[:, bass.ds(n, 1)], att_p[u % 2], ALU.mult, ALU.add)\
                    .then_inc(res_ready, 1)

            def attend(b, u, fb, ft):
                item = ft is not None
                if b is not None:
                    n, q, k = b * T + u, u % 2, SLOTS[u]
                    g3 = tile_at(u, ROW).rearrange("p (k c) -> p k c", c=ROW)
                    p3 = pr[:, 0:k * H].rearrange("p (k h) -> p k h", h=H)
                    if u:
                        combine(b, u - 1)
                    hold(dve, exp_ready, n + 1)
                    v.tensor_reduce(su[:, :], p3.rearrange("p k h -> p h k"), AX, ALU.add)
                settle()
                if b is not None:
                    v.reciprocal(su[:, :], su[:, :])
                if item:
                    hold(dve, elu_ready, fb * T + ft + 1)
                    v.scalar_tensor_tensor(y2[:, :], z[:, :], 0.0, neg[:, :], ALU.max, ALU.add)
                settle()
                if b is not None:
                    v.tensor_scalar(su[:, :], su[:, :], has_all[:, bass.ds(n, 1)], None, ALU.mult)
                if item:
                    v.scalar_tensor_tensor(y2[:, :], y2[:, :], -1.0, pair[ft % 2][:, C:2 * C],
                                           ALU.add, ALU.add).then_inc(pair_used, 1)
                settle()
                if b is not None:
                    v.tensor_tensor(p3, p3, su[:, :].unsqueeze(1).broadcast_to([P, k, H]), ALU.mult)
                if item:
                    if ft < T - 1:
                        wait_pair(fb, ft + 1)
                        v.bn_stats(stats[:, 0:6], pair[1 - ft % 2][:, 0:C])
                    v.bn_stats(stats[:, 6:12], y2[:, :])
                settle()
                if b is not None:
                    g4 = g3[:, :, 0:C].rearrange("p k (h d) -> p k h d", d=DH)
                    v.tensor_tensor(g4, g4, p3.unsqueeze(3).broadcast_to([P, k, H, DH]), ALU.mult)\
                        .then_inc(rows_weighted, 1)
                if item:
                    for j in range(0 if ft < T - 1 else 1, 2):
                        v.bn_aggr(mv[:, 2 * j:2 * j + 2], stats[:, 6 * j:6 * j + 6])
                    settle()
                    for j in range(0 if ft < T - 1 else 1, 2):
                        v.tensor_scalar(var[:, j:j + 1], mv[:, 2 * j + 1:2 * j + 2], EPS, None, ALU.add)
                    v.drain().then_inc(var_ready, 1)

            def wait_pair(b, t):
                hold(dve, pair_ld[t % 2], 16 * (B * T + b * T + t // 2 * 2 + 2))

            def last_norm(b):
                hold(dve, std_ready, B * T + (b + 1) * (T + 1))
                settle()
                v.reciprocal(rstd[:, :], std[:, :])
                hold(dve, final_out[1], 16 * (b * half + half - 1))
                settle()
                normal(x1[1][:, :], y2[:, :], 1).then_inc(final_ready, 1)

            def dense(b):
                hold(dve, dense_out, T * b)
                v.drain().then_inc(dense_go, 1)
                hold(dve, flag_ready, 2 * b + 2)
                many = dve.value_load(flag_i[0:1, bass.ds(2 * b + 1, 1)])
                with dve.If(many > 0):
                    with dve.Fori(0, T) as t:
                        n = b * T + t
                        hold(dve, dense_adj, n + 1)
                        hold(dve, dense_turn, 4 * H * n)
                        v.tensor_scalar(mask, adj_i[0][:, :], -FAR, FAR, ALU.mult, ALU.add)\
                            .then_inc(dense_mask, 1)
                        settle()
                        with dve.Fori(0, H) as h:
                            m = n * H + h
                            hold(dve, dense_turn, 4 * m)
                            hold(dve, dense_row, m + 1)
                            for g in range(2):
                                v.tensor_scalar(heat[:, 1024 * g:1024 * (g + 1)], score_p[g][:, :],
                                                self_s[:, bass.ds(m, 1)], None, ALU.add)
                            settle()
                            v.scalar_tensor_tensor(heat, heat, 0.2, heat, ALU.mult, ALU.max)
                            settle()
                            v.tensor_tensor(heat, heat, mask, ALU.add)
                            settle()
                            v.tensor_reduce(peak[:, :], heat, AX, ALU.max)
                            settle()
                            v.tensor_scalar(peak[:, :], peak[:, :], -1.0, None, ALU.mult)
                            v.drain().then_inc(dense_e, 1)
                        v.tensor_scalar(lone[:, 0:1], degree[:, bass.ds(n, 1)], 0.5, None, ALU.is_gt)
                        v.tensor_scalar(lone[:, 1:2], degree[:, bass.ds(n, 1)], 0.5, None, ALU.is_lt)
                        hold(dve, dense_att, H * (n + 1))
                        hold(dve, dense_out, n)
                        v.reciprocal(su[:, :], sums[:, :])
                        settle()
                        v.tensor_scalar(su[:, :], su[:, :], lone[:, 0:1], None, ALU.mult)
                        settle()
                        v.tensor_tensor(y[:, :].rearrange("p (h d) -> p h d", d=DH),
                                        sum_p[:, 0:C].rearrange("p (h d) -> p h d", d=DH),
                                        su[:, :].unsqueeze(2).broadcast_to([P, H, DH]), ALU.mult)
                        settle()
                        v.scalar_tensor_tensor(all_res[:, :], mean_wh[:, bass.ds(b * C, C)],
                                               lone[:, 1:2], y[:, :], ALU.mult, ALU.add)
                        v.drain().then_inc(dense_res, 1)
                with dve.Else():
                    dve.sem_inc(dense_mask, T)
                    dve.sem_inc(dense_e, T * H)
                    dve.sem_inc(dense_res, T)
                settle()

            def bridge():
                dve.wait_ge(mean_ready, 1)
                graph_terms(0)
                for u in range(T):
                    if u == LATE_AT:
                        late_lists(0, B)
                    if u:
                        finish_a(B - 1, u - 1)
                    weights(0, u, None, None)
                    if u:
                        finish_b(B - 1, u - 1)
                    attend(0, u, None, None)
                    if u == 0:
                        redo(B - 1)
                    if u == SORT_AT:
                        early_lists(1, B + 1)
                finish_a(B - 1, T - 1)
                finish_b(B - 1, T - 1)

            def stage2(b, reduce, finish):
                t_f = 0
                if reduce:
                    graph_terms(b)
                if isinstance(b, int) and b == B:
                    settle()
                combine(b - 1, T - 1)
                settle()
                dense(b - 1)
                rb = b if reduce else None
                for u in range(T):
                    if reduce and u == LATE_AT:
                        late_lists(b, B + b)
                    if FINISH[u] and not t_f:
                        wait_pair(b - 1, 0)
                        settle()
                        variance(pair[0][:, 0:C], 0)
                        v.drain().then_inc(var_ready, 1)
                    weights(rb, u, b - 1, t_f if FINISH[u] else None)
                    attend(rb, u, b - 1, t_f if FINISH[u] else None)
                    if FINISH[u]:
                        t_f += 1
                    for _ in range(1, FINISH[u]):
                        weights(None, u, b - 1, t_f)
                        attend(None, u, b - 1, t_f)
                        t_f += 1
                    if reduce and u == SORT_AT and not (isinstance(b, int) and b == B - 1):
                        early_lists(b + 1, B + b + 1)
                last_norm(b - 1)

            program(dve, stage1, bridge, stage2)


_INS = ["x", "adj", "L0_gnn_W", "L0_gnn_b", "L1_gnn_W", "L1_gnn_a1", "L1_gnn_a2",
        "L1_gnn_edge_emb", "L1_gnn_ln_gamma", "L1_gnn_ln_beta"]


def kernel(**inputs):
    import numpy as _np
    import concourse.bacc as _bacc
    from concourse import mybir as _mybir
    from concourse.bass_utils import run_bass_kernel_spmd as _run

    nc = _bacc.Bacc("TRN2", target_bir_lowering=False, num_devices=1)
    arrays, args = {}, []
    for name in _INS:
        a = _np.ascontiguousarray(inputs[name])
        arrays[f"in_{name}_dram"] = a
        args.append(nc.dram_tensor(f"in_{name}_dram", a.shape, _mybir.dt.from_np(a.dtype),
                                   kind="ExternalInput").ap())
    out = nc.dram_tensor("out_dram", (B, N, C), _mybir.dt.float32, kind="ExternalOutput").ap()
    build(nc, *args, out)
    r = _run(nc, [arrays], core_ids=[0])
    return r.results[0]["out_dram"]
```
